# Optimizing a Trainium2 kernel written in Bass

```python
import numpy as np
import jax
import jax.numpy as jnp

def _softmax(x, axis=-1):
    return jax.nn.softmax(x, axis=axis)

def _gelu(x):
    return jax.nn.gelu(x, approximate=True)

def _silu(x):
    return jax.nn.silu(x)

def _sigmoid(x):
    return jax.nn.sigmoid(x)

def _layernorm(x, axis=-1, eps=1e-05):
    m = jnp.mean(x, axis=axis, keepdims=True)
    v = jnp.var(x, axis=axis, keepdims=True)
    return (x - m) / jnp.sqrt(v + eps)

def _scatter_add(tgt, idx, src, axis=0):
    return tgt.at[idx].add(src)

def _segment_sum(src, seg, n):
    return jax.ops.segment_sum(src, seg, n)
kernel_name = 'mk_seq_postln_d1_jaxref_r4_88f30e'

def setup_inputs(seed: int=0):
    np.random.seed(seed)
    _w = jnp.asarray

    def _L0_attn_setup():
        import jax, jax.numpy as jnp
        import numpy as np
        import math
        DIM = 256
        NUM_HEADS = 16
        HEAD_DIM = DIM // NUM_HEADS
        MAX_BIAS = 8.0
        SCALE = HEAD_DIM ** (-0.5)

        def _alibi_slopes(n):

            def pow2(n):
                start = 2.0 ** (-2.0 ** (-(math.log2(n) - 3)))
                return [start * start ** i for i in range(n)]
            if math.log2(n).is_integer():
                return pow2(n)
            c = 2 ** math.floor(math.log2(n))
            return pow2(c) + _alibi_slopes(2 * c)[0::2][:n - c]

        def _rotate_half(t):
            t1, t2 = jnp.split(t, 2, axis=-1)
            return jnp.concatenate([-t2, t1], axis=-1)
        key = jax.random.key(seed)
        k1, k2, k3, k4 = jax.random.split(key, 4)
        B, N, C = (2, 512, DIM)
        x = jax.random.normal(k1, (B, N, C), dtype=jnp.float32)
        qkv_w = jax.random.normal(k2, (3 * C, C), dtype=jnp.float32) * C ** (-0.5)
        proj_w = jax.random.normal(k3, (C, C), dtype=jnp.float32) * C ** (-0.5)
        proj_b = jax.random.normal(k4, (C,), dtype=jnp.float32) * 0.01
        slopes = jnp.asarray(np.array(_alibi_slopes(NUM_HEADS), dtype=np.float32))
        return {'x': x, 'qkv_w': qkv_w, 'proj_w': proj_w, 'proj_b': proj_b, 'slopes': slopes}
    _L0_attn_in = _L0_attn_setup()

    def _L0_ffn_setup():
        import jax, jax.numpy as jnp
        import numpy as np
        E = 8
        K = 2
        key = jax.random.key(seed)
        ks = jax.random.split(key, 8)
        B, T, d = (4, 512, 256)
        h = 4 * d // E
        s = 0.02
        X = jax.random.normal(ks[0], (B, T, d), jnp.float32)
        routing_W = jax.random.normal(ks[1], (E, d), jnp.float32) * s
        expert_bias = jnp.zeros((E,), jnp.float32)
        sW1 = jax.random.normal(ks[2], (d, h), jnp.float32) * s
        sb1 = jnp.zeros((h,), jnp.float32)
        sW2 = jax.random.normal(ks[3], (h, d), jnp.float32) * s
        sb2 = jnp.zeros((d,), jnp.float32)
        rW1 = jax.random.normal(ks[4], (E, d, h), jnp.float32) * s
        rb1 = jnp.zeros((E, h), jnp.float32)
        rW2 = jax.random.normal(ks[5], (E, h, d), jnp.float32) * s
        rb2 = jnp.zeros((E, d), jnp.float32)
        return dict(X=X, routing_W=routing_W, expert_bias=expert_bias, sW1=sW1, sb1=sb1, sW2=sW2, sb2=sb2, rW1=rW1, rb1=rb1, rW2=rW2, rb2=rb2)
    _L0_ffn_in = _L0_ffn_setup()
    _d = {'L0_attn_x': _L0_attn_in['x'], 'L0_attn_qkv_w': _L0_attn_in['qkv_w'], 'L0_attn_proj_w': _L0_attn_in['proj_w'], 'L0_attn_proj_b': _L0_attn_in['proj_b'], 'L0_attn_slopes': _L0_attn_in['slopes'], 'L0_ffn_routing_W': _L0_ffn_in['routing_W'], 'L0_ffn_expert_bias': _L0_ffn_in['expert_bias'], 'L0_ffn_sW1': _L0_ffn_in['sW1'], 'L0_ffn_sb1': _L0_ffn_in['sb1'], 'L0_ffn_sW2': _L0_ffn_in['sW2'], 'L0_ffn_sb2': _L0_ffn_in['sb2'], 'L0_ffn_rW1': _L0_ffn_in['rW1'], 'L0_ffn_rb1': _L0_ffn_in['rb1'], 'L0_ffn_rW2': _L0_ffn_in['rW2'], 'L0_ffn_rb2': _L0_ffn_in['rb2']}
    _x0 = _d['L0_attn_x']
    _d['L0_attn_x'] = jax.random.normal(jax.random.fold_in(jax.random.key(seed), 1), (16, 512, 256), dtype=_x0.dtype)
    del _x0
    return _d

def reference(L0_attn_x, L0_attn_qkv_w, L0_attn_proj_w, L0_attn_proj_b, L0_attn_slopes, L0_ffn_routing_W, L0_ffn_expert_bias, L0_ffn_sW1, L0_ffn_sb1, L0_ffn_sW2, L0_ffn_sb2, L0_ffn_rW1, L0_ffn_rb1, L0_ffn_rW2, L0_ffn_rb2):

    def _L0_attn_ref(x, qkv_w, proj_w, proj_b, slopes):
        import jax, jax.numpy as jnp
        import numpy as np
        import math
        DIM = 256
        NUM_HEADS = 16
        HEAD_DIM = DIM // NUM_HEADS
        MAX_BIAS = 8.0
        SCALE = HEAD_DIM ** (-0.5)

        def _alibi_slopes(n):

            def pow2(n):
                start = 2.0 ** (-2.0 ** (-(math.log2(n) - 3)))
                return [start * start ** i for i in range(n)]
            if math.log2(n).is_integer():
                return pow2(n)
            c = 2 ** math.floor(math.log2(n))
            return pow2(c) + _alibi_slopes(2 * c)[0::2][:n - c]

        def _rotate_half(t):
            t1, t2 = jnp.split(t, 2, axis=-1)
            return jnp.concatenate([-t2, t1], axis=-1)
        B, N, C = x.shape
        H, D = (NUM_HEADS, HEAD_DIM)
        qkv = (x @ qkv_w.T).reshape(B, N, 3, H, D).transpose(2, 0, 3, 1, 4)
        q, k, v = (qkv[0], qkv[1], qkv[2])
        inv_freq = 1.0 / 10000.0 ** (jnp.arange(0, D, 2, dtype=jnp.float32) / D)
        freqs = jnp.arange(N, dtype=jnp.float32)[:, None] * inv_freq[None, :]
        sin = jnp.tile(jnp.sin(freqs), (1, 2))
        cos = jnp.tile(jnp.cos(freqs), (1, 2))
        q = q * cos + _rotate_half(q) * sin
        k = k * cos + _rotate_half(k) * sin
        attn = jnp.einsum('bhqd,bhkd->bhqk', q, k) * SCALE
        pos = jnp.arange(N, dtype=jnp.float32)
        diff = pos[None, :] - pos[:, None]
        diff = jnp.where(diff > 0, 0.0, diff)
        alibi = diff[None, :, :] * slopes[:, None, None] * MAX_BIAS
        attn = attn + alibi[None]
        w = jax.nn.softmax(attn, axis=-1)
        out = jnp.einsum('bhqk,bhkd->bhqd', w, v)
        out = out.transpose(0, 2, 1, 3).reshape(B, N, C)
        return out @ proj_w.T + proj_b

    def _L0_ffn_ref(X, routing_W, expert_bias, sW1, sb1, sW2, sb2, rW1, rb1, rW2, rb2):
        import jax, jax.numpy as jnp
        import numpy as np
        E = 8
        K = 2
        B, T, d = X.shape
        shared = jax.nn.silu(X @ sW1 + sb1) @ sW2 + sb2
        logits = jnp.einsum('btd,ed->bte', X, routing_W) + expert_bias
        activation = jnp.sqrt(jax.nn.softplus(logits))
        top_vals, top_idx = jax.lax.top_k(activation, K)
        combine = jnp.sum(jax.nn.one_hot(top_idx, E, dtype=X.dtype) * top_vals[..., None], axis=-2)
        Xf = X.reshape(-1, d)
        cf = combine.reshape(-1, E)
        hdn = jax.nn.silu(jnp.einsum('nd,edh->enh', Xf, rW1) + rb1[:, None, :])
        y = jnp.einsum('enh,ehd->end', hdn, rW2) + rb2[:, None, :]
        routed = jnp.einsum('ne,end->nd', cf, y).reshape(B, T, d)
        return shared + routed
    x = L0_attn_x
    x = _layernorm(x + _L0_attn_ref(x, L0_attn_qkv_w, L0_attn_proj_w, L0_attn_proj_b, L0_attn_slopes), axis=-1)
    x = _layernorm(x + _L0_ffn_ref(x, L0_ffn_routing_W, L0_ffn_expert_bias, L0_ffn_sW1, L0_ffn_sb1, L0_ffn_sW2, L0_ffn_sb2, L0_ffn_rW1, L0_ffn_rb1, L0_ffn_rW2, L0_ffn_rb2), axis=-1)
    return x

_drawn_inputs = setup_inputs


def setup_inputs(seed=0):
    import zlib

    import numpy as np

    out = dict(_drawn_inputs(seed))
    spreads = {'L0_ffn_expert_bias': (0.0, 0.1),
     'L0_ffn_sb1': (0.0, 0.732),
     'L0_ffn_sb2': (0.0, 0.1),
     'L0_ffn_rb1': (0.0, 0.501),
     'L0_ffn_rb2': (0.0, 0.1)}
    factors = {'L0_attn_proj_b': 4.119}
    for name, (base, spread) in spreads.items():
        noise = np.random.default_rng([zlib.crc32(name.encode()), seed]).standard_normal(out[name].shape)
        drawn = base * np.exp(spread * noise) if base else spread * noise
        out[name] = jnp.asarray(drawn.astype(out[name].dtype))
    for name, factor in factors.items():
        out[name] = (out[name] * factor).astype(out[name].dtype)
    return out
```

```python
from contextlib import ExitStack

import numpy as np
import concourse.bass as bass
from concourse import mybir

ALU = mybir.AluOpType
ACT = mybir.ActivationFunctionType
F32 = mybir.dt.float32
BF16 = mybir.dt.bfloat16
AX = mybir.AxisListType.X

NB, T, C = 16, 512, 256
H, D = 16, 16
E = 8
LAG = 28
PVLAG = 6
NTILE = NB * 64
ROWS = 116
EPS = 1e-5
QPART = (0, 0, 1, 1, 0, 2)
KPART = (0, 1, 0, 1, 2, 0)


class Done(dict):

    def get(self, k):
        return None if k < 0 else self[k]


class Queues:

    def __init__(self, nc, ctx):
        self.nc, self.ctx = nc, ctx
        self.sems, self.count = {}, {}
        self.todo = {e: [] for e in ("tensor", "vector", "scalar", "gpsimd", "sync")}

    def put(self, engine, fn, waits=(), sem=None, inc=1):
        if sem is not None and sem not in self.sems:
            self.sems[sem] = self.ctx.enter_context(self.nc.semaphore(sem))
            self.count[sem] = 0
        self.todo[engine].append((tuple(w for w in waits if w is not None), fn, sem, inc))
        if sem is None:
            return None
        self.count[sem] += inc
        return (sem, self.count[sem])

    def run(self, engine, eng):
        passed = {}
        for waits, fn, sem, inc in self.todo[engine]:
            for name, value in waits:
                if passed.get(name, 0) < value:
                    eng.wait_ge(self.sems[name], value)
                    passed[name] = value
            if fn is None:
                continue
            ins = fn(eng)
            if sem is not None:
                ins.then_inc(self.sems[sem], inc)


def build(nc, A, out):
    with ExitStack() as ctx:
        _build(nc, ctx, A, out)


def _build(nc, ctx, A, out):
    def sb(name, shape, dt=F32):
        return ctx.enter_context(nc.sbuf_tensor(name, shape, dt))

    def ps(name, shape, dt=F32):
        return ctx.enter_context(nc.psum_tensor(name, shape, dt))

    def dr(name, shape, dt):
        return nc.dram_tensor(name, shape, dt, kind="Internal").ap()

    q = Queues(nc, ctx)

    def pe(fn, *w, s=None):
        return q.put("tensor", fn, w, s)

    def dve(fn, *w, s=None):
        return q.put("vector", fn, w, s)

    def act(fn, *w, s=None):
        return q.put("scalar", fn, w, s)

    def pool(fn, *w, s=None):
        return q.put("gpsimd", fn, w, s)

    def dma(dst, src, *w, s, by="sync"):
        return q.put(by, lambda e: e.dma_start(dst, src), w, s, 16)

    qa = [sb(f"qa{i}", [128, 8, T], BF16) for i in range(3)]
    ka = [sb(f"ka{i}", [128, 8, T], BF16) for i in range(3)]
    ee = sb("ee", [128, 3, 4, T])
    vv = [sb(f"vv{i}", [128, 4, H, 32]) for i in range(2)]
    xT = sb("xT", [128, 2, T])
    wqkv = sb("wqkv", [128, 2, 768])
    wp = sb("wp", [128, 4, C])
    w1 = sb("w1", [128, 9, 2, 128])
    w2 = sb("w2", [128, 9, C])
    rw = sb("rw", [128, 2, E])
    b1 = sb("b1", [128, 9])
    hb1 = sb("hb1", [128, 9])
    ebb = sb("ebb", [128, 4, E])
    sb2 = sb("sb2", [128, C])
    rb2 = sb("rb2", [24, C])
    rb2p = sb("rb2p", [24, 3, C], BF16)
    rope = sb("rope", [128, 2, T])
    raw = sb("raw", [128, T])
    sh = sb("sh", [128, T])
    parts = [sb(f"parts{i}", [128, 3, T], BF16) for i in range(2)]
    idf = sb("idf", [128, 128])
    idb = sb("idb", [128, 128], BF16)
    tri = sb("tri", [128, 2, 128], BF16)
    mA = sb("mA", [128, 3, H, 128], BF16)
    mB = sb("mB", [128, 2, H, 128], BF16)
    sl = sb("sl", [128, H])
    slp = sb("slp", [128, 3, H])
    slq = sb("slq", [128, 3, H], BF16)
    negm = sb("negm", [128, 8, 4])
    mp = sb("mp", [128, 8, 2, 4], BF16)
    mrow = sb("mrow", [8, 4, 128], BF16)
    pvs = sb("pvs", [128, 4, T])
    rb = sb("rb", [128, 4, T])
    sc = sb("sc", [128, 64])
    scr = sb("scr", [128, 64])
    z = sb("z", [128, 4, C])
    x1 = sb("x1", [128, 4, C])
    x1T = sb("x1T", [128, 2, T])
    st = sb("st", [128, 2, 4, 6])
    mv = sb("mv", [128, 2, 4, 2])
    ve = sb("ve", [128, 2, 4])
    rs = sb("rs", [128, 2, 4])
    half = sb("half", [128, 2, 32])
    rr = sb("rr", [128, 12, 4, E])
    rm = sb("rm", [128, 4, 4])
    wkey = sb("wkey", [128, 4, E])
    cp = sb("cp", [128, 4, 3, E], BF16)
    cT = sb("cT", [24, T], BF16)
    sel = sb("sel", [24, E, 128], BF16)
    th = sb("th", [128, T])
    cf = sb("cf", [128, T])
    hs = [sb(f"hs{i}", [128, T]) for i in range(2)]

    pS = [ps(f"pS{i}", [128, T]) for i in range(2)]
    pT = [ps(f"pT{i}", [128, T]) for i in range(2)]
    pV = ps("pV", [128, T])
    pG = ps("pG", [128, T])
    pD = [ps(f"pD{i}", [128, 2, C]) for i in range(2)]
    pGb = pG[:, :].bitcast(BF16)

    d_part = [dr(f"d_part{i}", [2, 3, H, D, T], BF16) for i in range(2)]
    d_bias = dr("d_bias", [2, 3, 3, H, T], BF16)
    d_m = dr("d_m", [NB * H, 2, T], BF16)
    d_sum = [dr(f"d_sum{i}", [4, 4, T], F32) for i in range(2)]
    d_rec = [dr(f"d_rec{i}", [4, 4, T], F32) for i in range(2)]

    l_qkv = dma(wqkv[:, :, :], A["qkv_wT"].rearrange("(c p) n -> p c n", p=128), s="l_qkv")

    def load_xT(b, *w):
        return dma(xT[:, :, :], A["xT"].rearrange("(c p) n -> p c n", p=128)[:, :, b * T:(b + 1) * T], *w, s="l_xT")

    def load_x(b, *w):
        return dma(z[:, :, :], A["x"][b].rearrange("(t p) c -> p t c", p=128), *w, s="l_x")

    xT_in = load_xT(0)
    dma(rope[:, 0, :], A["k_cos"], s="l_rope")
    l_rope = dma(rope[:, 1, :], A["k_sin"], s="l_rope")
    dma(sl[:, :], A["slopes"].rearrange("(a h) -> a h", a=1).broadcast_to([128, H]), s="l_sl", by="scalar")
    l_sl = dma(tri[:, :, :], A["k_tri"], s="l_sl", by="scalar")
    pos = ee[:, 0, 0, 0:384]
    slc = sb("slc", [128, 1])
    dma(pos, A["k_pos"], s="l_pos", by="scalar")
    s_ap = A["slopes"].rearrange("(h a) -> h a", a=1)
    l_pos = None
    for h in range(H):
        l_pos = dma(slc[8 * h:8 * h + 8, :], s_ap[h:h + 1, :].broadcast_to([8, 1]), s="l_pos", by="scalar")
    l_ind = None
    for i in range(3):
        for h in range(8):
            dma(qa[i][96:105, h, :], A["k_qind"], s="l_ind", by="scalar")
            l_ind = dma(ka[i][105:116, h, :], A["k_kind"], s="l_ind", by="scalar")
    l_id = None
    for t_, n_ in ((idb[:, :], "k_idb"), (idf[:, :], "k_idf")):
        l_id = dma(t_, A[n_], s="l_id")
    x_in = load_x(0)
    dma(wp[:, :, :], A["wp"], s="l_w")
    dma(w1[:, :, :, :], A["w1"], s="l_w")
    dma(w2[:, :, :], A["w2"], s="l_w")
    dma(rw[:, :, :], A["rwT"].rearrange("(c p) e -> p c e", p=128), s="l_w")
    dma(b1[:, :], A["b1"], s="l_w")
    dma(sb2[:, :], A["sb2"].rearrange("(a c) -> a c", a=1).broadcast_to([128, C]), s="l_w")
    for t in range(4):
        dma(ebb[:, t, :], A["eb"].rearrange("(a c) -> a c", a=1).broadcast_to([128, E]), s="l_w")
    for p in range(3):
        dma(rb2[8 * p:8 * p + 8, :], A["rb2"], s="l_w")
    dma(sel[:, :, :], A["k_sel"], s="l_w")
    l_w = dma(wkey[:, :, :], A["k_key"], s="l_w")

    def link(fn, *w):
        return dve(fn, *w, s="s_link")

    ones = [dve(lambda e, i=i: e.memset(vv[i][:, :, :, 16:32], 1.0), s="s_set") for i in range(2)][-1]
    k = link(lambda e: e.tensor_scalar(slp[:, 0, :], sl[:, :], -32.0, None, ALU.mult), l_sl)
    k = link(lambda e: e.tensor_copy(slq[:, 0, :], slp[:, 0, :]), k)
    k = link(lambda e: e.tensor_tensor(slp[:, 1, :], slp[:, 0, :], slq[:, 0, :], ALU.subtract), k)
    k = link(lambda e: e.tensor_copy(slq[:, 1, :], slp[:, 1, :]), k)
    k = link(lambda e: e.tensor_tensor(slq[:, 2, :], slp[:, 1, :], slq[:, 1, :], ALU.subtract), k)

    def spread(dst, m, p):
        v = tri[:, m, :].rearrange("p (a j) -> p a j", a=1).broadcast_to([128, H, 128])
        c = slq[:, p, :].rearrange("p (h a) -> p h a", a=1).broadcast_to([128, H, 128])
        return dve(lambda e: e.tensor_tensor(dst, v, c, ALU.mult), k, s="s_set")

    for p in range(3):
        spread(mA[:, p, :, :], 1, p)
    for p in range(2):
        spread(mB[:, p, :, :], 0, p)
    pv_ = ee[:, 1, 0, 0:384]
    pb = parts[0]
    g0 = link(lambda e: e.tensor_scalar(pv_, pos, slc[:, 0:1], 32.0, ALU.mult, ALU.mult), l_pos)
    g1 = link(lambda e: e.tensor_copy(pb[:, 0, 0:384], pv_), g0)
    g2 = link(lambda e: e.tensor_tensor(pv_, pv_, pb[:, 0, 0:384], ALU.subtract), g1)
    g3 = link(lambda e: e.tensor_copy(pb[:, 1, 0:384], pv_), g2)
    g4 = link(lambda e: e.tensor_tensor(pb[:, 2, 0:384], pv_, pb[:, 1, 0:384], ALU.subtract), g3)
    b_w = None
    for p in range(3):
        for side in range(2):
            for r in range(3):
                b_w = dma(d_bias[side, r, p].rearrange("h (c e) -> (h c) e", c=8),
                          pb[:, p, (side * 3 + r) * 64:(side * 3 + r + 1) * 64], g4, s="b_w")
    l_bias = None

    def bias_rows(k_, *w):
        hs_ = slice((k_ % 2) * 8, (k_ % 2) * 8 + 8)
        dma(ka[k_ % 3][96:105, :, :], d_bias[0].rearrange("r p h t -> (r p) h t")[:, hs_, :], b_w, *w,
            s=f"qk_in{k_ % 3}")
        return dma(qa[k_ % 3][105:114, :, :], d_bias[1].rearrange("r p h t -> (r p) h t")[:, hs_, :], b_w, *w,
                   s=f"qk_in{k_ % 3}")

    dve(lambda e: e.memset(half[:, 0, :], -0.5), s="s_set")
    s_half = dve(lambda e: e.memset(half[:, 1, :], 0.5), s="s_set")
    k = link(lambda e: e.tensor_scalar(hb1[:, :], b1[:, :], 0.5, None, ALU.mult), l_w)
    k = link(lambda e: e.tensor_scalar(rb2[:, :], rb2[:, :], 2.0, None, ALU.mult), k)
    k = link(lambda e: e.tensor_copy(rb2p[:, 0, :], rb2[:, :]), k)
    k = link(lambda e: e.tensor_tensor(rb2[:, :], rb2[:, :], rb2p[:, 0, :], ALU.subtract), k)
    k = link(lambda e: e.tensor_copy(rb2p[:, 1, :], rb2[:, :]), k)
    k = link(lambda e: e.tensor_tensor(rb2p[:, 2, :], rb2[:, :], rb2p[:, 1, :], ALU.subtract), k)
    s_const = dve(lambda e: e.tensor_copy(rm[:, 0, :], half[:, 0, 0:4]), k, s="s_set")

    g_free = [None]
    last = {"raw": None, "sh": None, "parts": [b_w, None], "n": 0}
    v_ready = Done()
    st_done = Done()
    x1_state = Done()

    SWAP = [(i // 16) * 16 + (i % 16 + 8) % 16 for i in range(32)]

    def qk_tile(b, half_, side):
        col = side * 256 + half_ * 128
        for c in range(2):
            t = pe(lambda e, c=c: e.matmul(pG[:, :], wqkv[:, c, col:col + 128], xT[:, c, :], start=(c == 0),
                                           stop=(c == 1)),
                   l_qkv, xT_in_of[b], g_free[0], s="s_g" if c else None)
        i = last["n"] % 2
        last["n"] += 1
        unit = 2 * b + half_
        r = act(lambda e: e.copy(raw[:, :], pG[:, :]), t, last["raw"], s="s_raw")
        g_free[0] = r
        s_ = dve(lambda e: e.stream_shuffle(sh[:, :], raw[:, :], SWAP), r, last["sh"], s="s_sh")
        P = parts[i]
        a = pool(lambda e: e.tensor_tensor(raw[:, :], raw[:, :], rope[:, 0, :], ALU.mult), s_, l_rope, s="s_rope")
        a = pool(lambda e: e.tensor_tensor(sh[:, :], sh[:, :], rope[:, 1, :], ALU.mult), s_, s="s_rope")
        a = pool(lambda e: e.tensor_tensor(raw[:, :], raw[:, :], sh[:, :], ALU.add), a, s="s_rope")
        last["sh"] = a
        a = pool(lambda e: e.tensor_scalar(P[:, 0, :], raw[:, :], 1.0, None, ALU.mult), a, last["parts"][i],
                 s="s_rope")
        a = pool(lambda e: e.tensor_tensor(raw[:, :], raw[:, :], P[:, 0, :], ALU.subtract), a, s="s_rope")
        a = pool(lambda e: e.tensor_scalar(P[:, 1, :], raw[:, :], 1.0, None, ALU.mult), a, s="s_rope")
        a = pool(lambda e: e.tensor_tensor(P[:, 2, :], raw[:, :], P[:, 1, :], ALU.subtract), a, s="s_rope")
        last["raw"] = a
        hs_ = slice(half_ * 8, half_ * 8 + 8)
        w = None
        for p in range(3):
            w = dma(d_part[b % 2][side, p, hs_].rearrange("h d t -> (h d) t"), P[:, p, :], a, qk_in.get(unit - 4),
                    s=f"p_w{i}")
        last["parts"][i] = w
        part_in[unit, side] = w

    def assemble(unit):
        free = st_done.get(unit - 3)
        bias_rows(unit, free)
        hs_ = slice((unit % 2) * 8, (unit % 2) * 8 + 8)
        for side in range(2):
            dst = (qa, ka)[side][unit % 3]
            for n, p in enumerate((QPART, KPART)[side]):
                qk_in[unit] = dma(dst[16 * n:16 * n + 16, :, :],
                                  d_part[unit // 2 % 2][side, p, hs_].rearrange("h d t -> d h t"),
                                  part_in[unit, side], free, s=f"qk_in{unit % 3}")

    def v_tiles(b, j):
        for t in range(2):
            for c in range(2):
                tk = pe(lambda e, c=c, t=t: e.matmul(pG[:, t * C:(t + 1) * C],
                                                     xT[:, c, (2 * j + t) * 128:(2 * j + t + 1) * 128],
                                                     wqkv[:, c, 512:768], start=(c == 0), stop=(c == 1)),
                        xT_in_of[b], g_free[0], s="s_g" if (t and c) else None)
        r = act(lambda e: e.copy(vv[b % 2][:, 2 * j:2 * j + 2, :, 0:16],
                                 pG[:, :].rearrange("p (k h d) -> p k h d", k=2, h=H)),
                tk, pv_done.get(4 * (b - 2) + 3), ones, s="s_v")
        g_free[0] = r
        v_ready[b] = r
        return tk

    xT_in_of = Done({0: xT_in})
    qk_in, part_in = Done(), Done()
    pv_done = Done()
    xr_in = Done({0: x_in})

    def qkv_job(b, n):
        if n < 4:
            qk_tile(b, n // 2, n % 2)
        else:
            tk = v_tiles(b, n - 4)
            if n == 5 and b + 1 < NB:
                xT_in_of[b + 1] = load_xT(b + 1, tk)

    s_max, s_exp, s_ev = Done(), Done(), Done()
    m_in = Done()
    m_head = Done()

    def s_tile(s):
        b, h, t = s // 64, (s // 4) % 16, s % 4
        unit, hu = s // 32, h % 8
        bank = pS[s % 2]
        qs = slice(t * 128, t * 128 + 128)
        pe(lambda e: e.matmul(bank[:, :], qa[unit % 3][0:114, hu, qs], ka[unit % 3][0:114, hu, :], start=True, stop=False),
           qk_in[unit], l_ind, s_max.get(s - 2))
        for p in range(2):
            tk = pe(lambda e, p=p: e.matmul(bank[:, qs], tri[:, 1, :], mB[:, p, h, :], start=False, stop=(p == 1)),
                    s_const, s="s_s" if p else None)
        n = s // 4
        s_max[s] = dve(lambda e: e.tensor_reduce(negm[:, n % 8, t:t + 1], bank[:, :], AX, ALU.max, negate=True), tk,
                       m_head.get(n - 8), s="s_max")
        if t == 3:
            a = dve(lambda e: e.tensor_copy(mp[:, n % 8, 0, :], negm[:, n % 8, :]), s_max[s], m_head.get(n - 8),
                    s="s_mp")
            m_split[n] = dve(lambda e: e.tensor_tensor(mp[:, n % 8, 1, :], negm[:, n % 8, :], mp[:, n % 8, 0, :],
                                                       ALU.subtract), a, s="s_mp")

    m_split = Done()
    m_put = Done()

    def m_rows(n):
        b, h = n // 16, n % 16
        tk = pe(lambda e: e.transpose(pGb[0:8, 0:128], mp[:, n % 8, :, :].rearrange("p a t -> p (a t)"), idb[:, :]),
                m_split[n], g_free[0], l_id, s="s_g")
        m_head[n] = tk
        r = act(lambda e: e.copy(mrow[:, n % 4, :], pGb[0:8, 0:128]), tk, m_put.get(n - 4), s="s_mrow")
        g_free[0] = r
        w = dma(d_m[n].rearrange("p (t q) -> (p t) q", t=4), mrow[:, n % 4, :], r, s=f"m_w{n % 4}")
        m_put[n] = w
        m_in[n] = dma(qa[n // 8 % 3][114:116, h % 8, :], d_m[n], w, st_done.get(n // 8 - 3), s=f"m_in{n % 8}")

    def st_tile(u):
        g, kt, hh = u // 16, (u % 16) // 4, u % 4
        b, h = g // 4, (g % 4) * 4 + hh
        unit, hu = u // 32, h % 8
        bank = pT[u % 2]
        ks = slice(kt * 128, kt * 128 + 128)
        pe(lambda e: e.matmul(bank[:, :], ka[unit % 3][0:ROWS, hu, ks], qa[unit % 3][0:ROWS, hu, :], start=True, stop=False),
           m_in[g * 4 + hh], s_exp.get(u - 2))
        for p in range(3):
            tk = pe(lambda e, p=p: e.matmul(bank[:, ks], tri[:, 0, :], mA[:, p, h, :], start=False, stop=(p == 2)),
                    s="s_t" if p == 2 else None)
        if u % 32 == 31:
            st_done[unit] = tk
        w = u // 4
        s_exp[u] = act(lambda e: e.activation(ee[:, w % 3, hh, :], bank[:, :], ACT.Exp, scale=0.25), tk,
                       pv_quad.get(w - 3), g4, s="s_exp")

    pv_quad = Done()
    rec_done = Done()
    att_done = Done()

    def pv_step(w):
        g, kt = w // 4, w % 4
        b = g // 4
        for hh in range(4):
            h = (g % 4) * 4 + hh
            tk = pe(lambda e, hh=hh, h=h: e.matmul(pV[32 * hh:32 * hh + 32, :], vv[b % 2][:, kt, h, :],
                                                   ee[:, w % 3, hh, :], start=(kt == 0), stop=(kt == 3)),
                    s_exp[4 * w + 3], v_ready[b], s_ev.get(g - 1), s="s_pv" if hh == 3 else None)
        pv_quad[w] = tk
        if kt == 3:
            pv_done[g] = tk
            s_ev[g] = act(lambda e: e.copy(pvs[:, g % 4, :], pV[:, :]), tk, proj_done.get(b - 1), s="s_ev")
            if g % 4 == 3:
                normalise(b)

    proj_done = Done()

    def normalise(b):
        a = dma(d_sum[b % 2].rearrange("k g t -> k g t"), pvs[16:128:32, :, :], s_ev[4 * b + 3], s="sum_w")
        a = dma(sc[:, :], d_sum[b % 2].rearrange("k g (c e) -> (k g c) e", e=64), a, s="sum_in")
        sums[b] = a

    sums = Done()

    def reciprocals(b):
        a = dve(lambda e: e.reciprocal(scr[:, :], sc[:, :]), sums[b], s="s_rec")
        a = dma(d_rec[b % 2].rearrange("k g (c e) -> (k g c) e", e=64), scr[:, :], a, s="rec_w")
        for hh in range(4):
            rec_done[b] = dma(rb[32 * hh:32 * hh + 32, :, :],
                              d_rec[b % 2][hh:hh + 1].broadcast_to([32, 4, T]), a, att_done.get(b - 1), s="rec_in")

    def scale_att(b, g):
        att_done[b] = dve(lambda e: e.tensor_tensor(pvs[:, g, :], pvs[:, g, :], rb[:, g, :], ALU.mult), rec_done[b],
                          s="s_att")

    z_in = Done()
    out_w = Done()

    def proj_job(b, j):
        for t in range(2):
            for g in range(4):
                tk = pe(lambda e, t=t, g=g: e.matmul(pG[:, t * C:(t + 1) * C],
                                                     pvs[:, g, (2 * j + t) * 128:(2 * j + t + 1) * 128],
                                                     wp[:, g, :], start=(g == 0), stop=(g == 3)),
                        att_done[b], l_w, g_free[0], s="s_g" if (t and g == 3) else None)
        if j == 1:
            proj_done[b] = tk
        zz = z[:, 2 * j:2 * j + 2, :].rearrange("p t c -> p (t c)")
        z_in[b, j] = dve(lambda e: e.tensor_tensor(zz, pG[:, :], zz, ALU.add), tk, xr_in[b], s="s_z")
        g_free[0] = z_in[b, j]
        for t in (2 * j, 2 * j + 1):
            stats[b, 0, t] = dve(lambda e, t=t: e.bn_stats(st[:, 0, t, :], z[:, t, :]), z_in[b, j], s="s_st")

    stats = Done()

    def rstd(b, k):
        a = None
        for t in range(4):
            a = dve(lambda e, t=t: e.bn_aggr(mv[:, k, t, :], st[:, k, t, :]), stats[b, k, t], s="s_st")
        a = link(lambda e: e.tensor_scalar(ve[:, k, :], mv[:, k, :, 1], EPS, None, ALU.add), a)
        return pool(lambda e: e.tensor_tensor(rs[:, k, :], ve[:, k, :], half[:, 0, 0:4], ALU.pow), a, s_half,
                    s="s_pow")

    def norm1(b):
        a = rstd(b, 0)
        for t in range(4):
            n = dve(lambda e, t=t: e.tensor_scalar(x1[:, t, :], z[:, t, :], mv[:, 0, t, 0:1], rs[:, 0, t:t + 1],
                                                   ALU.subtract, ALU.mult), a, x1_state.get(b - 1), s="s_x1")
        x1_in[b] = n

    x1_in, x1T_in, ffn_read = Done(), Done(), Done()

    def turn_job(b, c):
        for t in range(4):
            tk = pe(lambda e, t=t: e.transpose(pG[:, t * 128:t * 128 + 128], x1[:, t, c * 128:c * 128 + 128],
                                               idf[:, :]), x1_in[b], g_free[0], s="s_g" if t == 3 else None)
        r = act(lambda e: e.copy(x1T[:, c, :], pG[:, :]), tk, ffn_read.get(b - 1), s="s_x1T")
        g_free[0] = r
        x1T_in[b] = r
        if c == 1:
            for t in range(4):
                r = pool(lambda e, t=t: e.tensor_tensor(x1[:, t, :], x1[:, t, :], sb2[:, :], ALU.add), tk, l_w,
                         s="s_x1b")
            x1b[b] = r

    x1b = Done()

    def route_job(b):
        for t in range(4):
            for c in range(2):
                tk = pe(lambda e, t=t, c=c: e.matmul(pG[:, 8 * t:8 * t + 8], x1T[:, c, t * 128:t * 128 + 128],
                                                     rw[:, c, :], start=(c == 0), stop=(c == 1)),
                        x1T_in[b], g_free[0], s="s_g" if (t == 3 and c) else None)
        a = link(lambda e: e.tensor_tensor(R(0), pG[:, 0:32].rearrange("p (t e) -> p t e", t=4), ebb[:, :, :],
                                           ALU.add), tk, cp_read.get(b - 1))
        g_free[0] = a
        a = link(lambda e: e.tensor_scalar(R(1), R(0), -1.0, None, ALU.mult), a)
        a = link(lambda e: e.tensor_tensor(R(2), R(0), R(1), ALU.min), a)
        a = act(lambda e: e.activation(R(3), R(2), ACT.Exp), a, s="s_u")
        route_u[b] = a

    def R(i):
        return rr[:, i, :, :]

    def RB(i):
        return rm[:, i, :].rearrange("p (t a) -> p t a", a=1).broadcast_to([128, 4, E])

    route_u, cp_read, route_a, route_c = Done(), Done(), Done(), Done()

    def route_softplus(b):
        a = link(lambda e: e.tensor_scalar(R(1), R(3), 2.0, None, ALU.add), route_u[b])
        a = link(lambda e: e.reciprocal(R(2), R(1)), a)
        a = link(lambda e: e.tensor_tensor(R(4), R(3), R(2), ALU.mult), a)
        a = link(lambda e: e.tensor_tensor(R(5), R(4), R(4), ALU.mult), a)
        a = link(lambda e: e.tensor_scalar(R(6), R(5), 1.0 / 17, None, ALU.mult), a)
        for n in (15, 13, 11, 9, 7, 5, 3):
            a = link(lambda e, n=n: e.scalar_tensor_tensor(R(6), R(6), 1.0 / n, R(5), ALU.add, ALU.mult), a)
        a = link(lambda e: e.scalar_tensor_tensor(R(6), R(6), 1.0, R(4), ALU.add, ALU.mult), a)
        a = link(lambda e: e.tensor_scalar(R(1), R(0), 0.0, None, ALU.max), a)
        a = link(lambda e: e.scalar_tensor_tensor(R(6), R(6), 2.0, R(1), ALU.mult, ALU.add), a)
        route_a[b] = pool(lambda e: e.tensor_tensor(R(7).rearrange("p t e -> p (t e)"),
                                                    R(6).rearrange("p t e -> p (t e)"), half[:, 1, :], ALU.pow), a,
                          s="s_pow")

    def route_top2(b):
        a = route_a[b]
        src = 7
        for n in range(2):
            a = link(lambda e, src=src: e.tensor_reduce(rm[:, 0, :], R(src), AX, ALU.max), a)
            a = link(lambda e, src=src: e.tensor_tensor(R(1), R(src), RB(0), ALU.is_equal), a)
            a = link(lambda e: e.tensor_tensor(R(2), R(1), wkey[:, :, :], ALU.mult), a)
            a = link(lambda e: e.tensor_reduce(rm[:, 1, :], R(2), AX, ALU.max), a)
            a = link(lambda e, n=n: e.tensor_tensor(R(8 + n), R(2), RB(1), ALU.is_equal), a)
            if n == 0:
                a = link(lambda e: e.scalar_tensor_tensor(R(11), R(8), -1e30, R(7), ALU.mult, ALU.add), a)
                src = 11
        a = link(lambda e: e.tensor_tensor(R(10), R(8), R(9), ALU.add), a)
        a = link(lambda e: e.scalar_tensor_tensor(R(10), R(10), 0.5, R(7), ALU.mult, ALU.mult), a)
        a = link(lambda e: e.tensor_copy(cp[:, :, 0, :], R(10)), a)
        a = link(lambda e: e.tensor_tensor(R(10), R(10), cp[:, :, 0, :], ALU.subtract), a)
        a = link(lambda e: e.tensor_copy(cp[:, :, 1, :], R(10)), a)
        route_c[b] = link(lambda e: e.tensor_tensor(cp[:, :, 2, :], R(10), cp[:, :, 1, :], ALU.subtract), a)

    cT_in = Done()

    def cT_job(b):
        for t in range(4):
            tk = pe(lambda e, t=t: e.transpose(pGb[0:24, t * 128:t * 128 + 128],
                                               cp[:, t, :, :].rearrange("p a e -> p (a e)"), idb[:, :]),
                    route_c[b], g_free[0], s="s_g" if t == 3 else None)
        cp_read[b] = tk
        r = act(lambda e: e.copy(cT[:, :], pGb[0:24, 0:T]), tk, ffn_read.get(b - 1), s="s_cT")
        g_free[0] = r
        cT_in[b] = r

    cf_in, hs_in, down = Done(), Done(), Done()
    a_done = Done()

    def cf_job(b, e_):
        n = 9 * b + e_
        tk = pe(lambda e: e.matmul(pG[:, :], sel[:, e_ - 1, :], cT[:, :], start=True, stop=True), cT_in[b],
                g_free[0], s="s_g")
        r = act(lambda e: e.copy(cf[:, :], pG[:, :]), tk, a_done.get(n - 1), s="s_cf")
        g_free[0] = r
        cf_in[n] = r

    def up_job(b, e_):
        n = 9 * b + e_
        for c in range(2):
            tk = pe(lambda e, c=c: e.matmul(pG[:, :], w1[:, e_, c, :], x1T[:, c, :], start=(c == 0), stop=(c == 1)),
                    x1T_in[b], l_w, g_free[0], s="s_g" if c else None)
        r = act(lambda e: e.activation(th[:, :], pG[:, :], ACT.Tanh, bias=hb1[:, e_:e_ + 1], scale=0.5), tk, s_const,
                hs_in.get(n - 1), s="s_th")
        if e_ == 0:
            a = dve(lambda e: e.tensor_scalar(hs[n % 2][:, :], pG[:, :], b1[:, 0:1], 0.5, ALU.add, ALU.mult), tk, r,
                    down.get(n - 2), s="s_a")
        else:
            a = dve(lambda e: e.scalar_tensor_tensor(hs[n % 2][:, :], pG[:, :], b1[:, e_:e_ + 1], cf[:, :],
                                                     ALU.add, ALU.mult), tk, r, cf_in[n], down.get(n - 2), s="s_a")
        a_done[n] = a
        g_free[0] = a
        hs_in[n] = dve(lambda e: e.scalar_tensor_tensor(hs[n % 2][:, :], th[:, :], 1.0, hs[n % 2][:, :], ALU.add,
                                                              ALU.mult), a, r, s="s_hs")

    z2_in = Done()

    def down_job(b, e_):
        n = 9 * b + e_
        for t in range(4):
            tk = pe(lambda e, t=t: e.matmul(pD[t // 2][:, t % 2, :], hs[n % 2][:, t * 128:t * 128 + 128],
                                            w2[:, e_, :], start=(e_ == 0 and t % 2 == 0), stop=False,
                                            skip_group_check=True),
                    hs_in[n], z2_in.get(b - 1), s="s_d" if t == 3 else None)
        down[n] = tk
        if e_ == 8:
            for t in range(4):
                for p in range(3):
                    tk = pe(lambda e, t=t, p=p: e.matmul(pD[t // 2][:, t % 2, :], cT[:, t * 128:t * 128 + 128],
                                                         rb2p[:, p, :], start=False, stop=(p == 2),
                                                         skip_group_check=True),
                            s_const, s="s_d" if (t == 3 and p == 2) else None)
            ffn_read[b] = tk
            for j in range(2):
                zz = z[:, 2 * j:2 * j + 2, :].rearrange("p t c -> p (t c)")
                xx = x1[:, 2 * j:2 * j + 2, :].rearrange("p t c -> p (t c)")
                z2_in[b] = dve(lambda e, j=j, zz=zz, xx=xx: e.tensor_tensor(
                    zz, pD[j][:, :, :].rearrange("p t c -> p (t c)"), xx, ALU.add), tk, x1b[b], s="s_z2")
                for t in (2 * j, 2 * j + 1):
                    stats[b, 1, t] = dve(lambda e, t=t: e.bn_stats(st[:, 1, t, :], z[:, t, :]), z2_in[b], s="s_st")
            x1_state[b] = z2_in[b]

    def finish(b):
        a = rstd(b, 1)
        for t in range(4):
            n = dve(lambda e, t=t: e.tensor_scalar(z[:, t, :], z[:, t, :], mv[:, 1, t, 0:1], rs[:, 1, t:t + 1],
                                                   ALU.subtract, ALU.mult), a, s="s_o")
        out_w[b] = dma(out[b].rearrange("(t p) c -> p t c", p=128), z[:, :, :], n, s="out_w")
        if b + 1 < NB:
            xr_in[b + 1] = load_x(b + 1, out_w[b])

    plan = {}

    def at(slot, fn, *a):
        plan.setdefault(slot, []).append((fn, a))

    taken = set()

    def job(slot, fn, *a):
        while slot in taken or (slot % 4 == 3):
            slot += 1
        taken.add(slot)
        at(slot, fn, *a)
        return slot

    for b in range(NB):
        o = 64 * b
        if b + 1 < NB:
            at(o + 42, assemble, 2 * b + 2)
            at(o + 62, assemble, 2 * b + 3)
        if b + 1 < NB:
            for n, w in enumerate((24, 28, 32, 38, 44, 46)):
                job(o + w, qkv_job, b + 1, n)
        e0 = o + LAG + 60 + PVLAG
        at(e0 + 3, reciprocals, b)
        for g in range(4):
            at(e0 + 7 + g // 2, scale_att, b, g)
        p = job(e0 + 9, proj_job, b, 0)
        p = job(p + 2, proj_job, b, 1)
        at(p + 1, norm1, b)
        p = job(p + 5, turn_job, b, 0)
        p = job(p + 1, turn_job, b, 1)
        p = job(p + 2, route_job, b)
        at(p + 1, route_softplus, b)
        u = job(p + 1, up_job, b, 0)
        at(u + 4, down_job, b, 0)
        at(p + 8, route_top2, b)
        p = job(p + 11, cT_job, b)
        for e_ in range(1, 9):
            p = job(p + 1, cf_job, b, e_)
            p = job(p + 1, up_job, b, e_)
            at(p + 3, down_job, b, e_)
        at(p + 7, finish, b)

    for n in range(6):
        qkv_job(0, n)
        if n in (1, 3):
            assemble(n // 2)
    for s in range(max(plan) + 1):
        if s < NTILE:
            s_tile(s)
        if 0 <= s - LAG < NTILE:
            st_tile(s - LAG)
        if s >= 7 and s % 4 == 3 and (s - 7) // 4 < NB * H:
            m_rows((s - 7) // 4)
        v = s - LAG - PVLAG
        if v >= 0 and v % 4 == 0 and v // 4 < NTILE // 4:
            pv_step(v // 4)
        for fn, a in plan.get(s, ()):
            fn(*a)
    q.put("sync", None, (out_w[NB - 1],))

    block = ctx.enter_context(nc.Block())

    @block.sync
    def _(e):
        q.run("sync", e)

    @block.tensor
    def _(e):
        q.run("tensor", e)

    @block.vector
    def _(e):
        q.run("vector", e)

    @block.scalar
    def _(e):
        q.run("scalar", e)

    @block.gpsimd
    def _(e):
        q.run("gpsimd", e)


def tables():
    bf = mybir.dt.np(BF16)
    f = np.float32
    t = {}
    inv = (f(1.0) / (f(10000.0) ** (np.arange(0, D, 2, dtype=f) / f(D)))).astype(f)
    fr = (np.arange(T, dtype=f)[:, None] * inv[None, :]).astype(f)
    row = np.arange(128) % D
    t["k_cos"] = np.ascontiguousarray(np.cos(fr).astype(f)[:, row % 8].T)
    sign = np.where(row < 8, f(-1), f(1))[:, None]
    t["k_sin"] = np.ascontiguousarray(np.sin(fr).astype(f)[:, row % 8].T * sign)
    j = np.arange(128)
    t["k_tri"] = np.stack([(j[None, :] <= j[:, None]), (j[:, None] < j[None, :])], 1).astype(bf)
    x = np.arange(T)
    kv = np.stack([(x - 128 * (r + 1)) * (x // 128 == r) for r in range(3)])
    qv = np.stack([-(x - 128 * (r + 1)) * (x // 128 > r) for r in range(3)])
    pos = np.stack([kv, qv]).reshape(6, 8, 64).transpose(1, 0, 2).reshape(8, 384)
    t["k_pos"] = np.tile(pos, (16, 1)).astype(f)
    t["k_qind"] = np.repeat(np.stack([x // 128 > r for r in range(3)]), 3, 0).astype(bf)
    t["k_kind"] = np.concatenate([np.repeat(np.stack([x // 128 == r for r in range(3)]), 3, 0),
                                  np.ones((2, T), bool)]).astype(bf)
    t["k_idb"] = np.eye(128).astype(bf)
    t["k_idf"] = np.eye(128, dtype=f)
    s = np.zeros((24, E, 128), f)
    for p in range(3):
        for e in range(E):
            s[8 * p + e, e] = 1
    t["k_sel"] = s.astype(bf)
    t["k_key"] = np.broadcast_to((8 - np.arange(E)).astype(f), (128, 4, E)).copy()
    return t


def kernel(**inputs):
    import concourse.bacc as _bacc
    from concourse.bass_utils import run_bass_kernel_spmd as _run

    i = {n: np.asarray(a) for n, a in inputs.items()}
    x = i["L0_attn_x"]
    a = {"x": x, "xT": x.reshape(NB * T, C).T, "qkv_wT": i["L0_attn_qkv_w"].T, "slopes": i["L0_attn_slopes"]}
    wp = np.zeros((4, 4, 32, C), np.float32)
    wp[:, :, 0:16, :] = i["L0_attn_proj_w"].T.reshape(4, 4, 16, C)
    wp[0, 0, 16, :] = i["L0_attn_proj_b"]
    a["wp"] = wp.transpose(1, 2, 0, 3).reshape(128, 4, C)
    w1 = np.concatenate([i["L0_ffn_sW1"][None], i["L0_ffn_rW1"]])
    a["w1"] = w1.reshape(9, 2, 128, 128).transpose(2, 0, 1, 3)
    a["w2"] = np.concatenate([i["L0_ffn_sW2"][None], i["L0_ffn_rW2"]]).transpose(1, 0, 2)
    a["b1"] = np.concatenate([i["L0_ffn_sb1"][None], i["L0_ffn_rb1"]]).T
    a["rwT"] = i["L0_ffn_routing_W"].T
    a["eb"] = i["L0_ffn_expert_bias"]
    a["sb2"] = i["L0_ffn_sb2"]
    a["rb2"] = i["L0_ffn_rb2"]
    a.update(tables())
    nc = _bacc.Bacc("TRN2", target_bir_lowering=False, num_devices=1)
    arrays, aps = {}, {}
    for n, v in a.items():
        v = np.ascontiguousarray(v)
        arrays["in_" + n] = v
        aps[n] = nc.dram_tensor("in_" + n, v.shape, mybir.dt.from_np(v.dtype), kind="ExternalInput").ap()
    out = nc.dram_tensor("out_0", (NB, T, C), F32, kind="ExternalOutput").ap()
    build(nc, aps, out)
    r = _run(nc, [arrays], core_ids=[0])
    return r.results[0]["out_0"]
```

```python
from contextlib import ExitStack

import numpy as np
import concourse.bass as bass
from concourse import mybir

ALU = mybir.AluOpType
ACT = mybir.ActivationFunctionType
F32 = mybir.dt.float32
BF16 = mybir.dt.bfloat16
F16 = mybir.dt.float16
AX = mybir.AxisListType.X

NB, T, C = 16, 512, 256
H, D = 16, 16
E = 8
LAG = 26
PVLAG = 6
NTILE = NB * 64
ROWS = 116
EPS = 1e-5
RATE = 1250
STEP = 1600
QK_GAP = 8000
URGENT = 16
LINKS = 6
TOP = 4
DOWN = 2.5
QK_AT = -8
V_AT = 44
QPART = (0, 0, 1, 1, 0, 2)
KPART = (0, 1, 0, 1, 2, 0)


class Done(dict):

    def get(self, k):
        return None if k < 0 else self[k]


class Queues:

    def __init__(self, nc, ctx):
        self.nc, self.ctx = nc, ctx
        self.sems, self.count = {}, {}
        self.todo = {e: [] for e in ("tensor", "vector", "scalar", "gpsimd", "sync")}

    def put(self, engine, fn, waits=(), sem=None, inc=1):
        if sem is not None and sem not in self.sems:
            self.sems[sem] = self.ctx.enter_context(self.nc.semaphore(sem))
            self.count[sem] = 0
        self.todo[engine].append((tuple(w for w in waits if w is not None), fn, sem, inc))
        if sem is None:
            return None
        self.count[sem] += inc
        return (sem, self.count[sem])

    def run(self, engine, eng):
        passed = {}
        for waits, fn, sem, inc in self.todo[engine]:
            for name, value in waits:
                if passed.get(name, 0) < value:
                    eng.wait_ge(self.sems[name], value)
                    passed[name] = value
            if fn is None:
                continue
            ins = fn(eng)
            if sem is not None:
                ins.then_inc(self.sems[sem], inc)


def build(nc, A, out):
    with ExitStack() as ctx:
        _build(nc, ctx, A, out)


def _build(nc, ctx, A, out):
    def sb(name, shape, dt=F32):
        return ctx.enter_context(nc.sbuf_tensor(name, shape, dt))

    def ps(name, shape, dt=F32):
        return ctx.enter_context(nc.psum_tensor(name, shape, dt))

    def dr(name, shape, dt):
        return nc.dram_tensor(name, shape, dt, kind="Internal").ap()

    q = Queues(nc, ctx)

    def pe(fn, *w, s=None):
        return q.put("tensor", fn, w, s)

    load = {"vector": 0, "scalar": 0}

    def dve(fn, *w, s=None, cost=110):
        load["vector"] += cost
        return q.put("vector", fn, w, s)

    def act(fn, *w, s=None, cost=560):
        load["scalar"] += cost
        return q.put("scalar", fn, w, s)

    def pool(fn, *w, s=None):
        return q.put("gpsimd", fn, w, s)

    def dma(dst, src, *w, s, by="sync"):
        return q.put(by, lambda e: e.dma_start(dst, src), w, s, 16)

    qa = [sb(f"qa{i}", [128, 8, T], BF16) for i in range(3)]
    ka = [sb(f"ka{i}", [128, 8, T], BF16) for i in range(3)]
    ee = sb("ee", [128, 3, 4, T])
    vv = [sb(f"vv{i}", [128, 4, H, 32]) for i in range(2)]
    xT = sb("xT", [128, 2, T])
    wqkv = sb("wqkv", [128, 2, 768])
    wp = sb("wp", [128, 4, C])
    w1 = sb("w1", [128, 9, 2, 128])
    w2 = sb("w2", [128, 9, C])
    rw = sb("rw", [128, 2, 32])
    b1 = sb("b1", [128, 9])
    ebb = sb("ebb", [128, 4, E])
    sb2 = sb("sb2", [128, C])
    rb2 = sb("rb2", [E, C])
    rope = sb("rope", [128, 2, T])
    raw = sb("raw", [128, T])
    sh = sb("sh", [128, T])
    parts = [sb(f"parts{i}", [128, 3, T], BF16) for i in range(2)]
    idf = sb("idf", [128, 128])
    tri = sb("tri", [128, 2, 128], BF16)
    mA = sb("mA", [128, 2, H, 128], F16)
    mB = sb("mB", [128, H, 128], F16)
    sl = sb("sl", [128, H])
    slp = sb("slp", [128, 2, H])
    slq = sb("slq", [128, 2, H], F16)
    negm = sb("negm", [128, 2, 4, 4])
    mp = sb("mp", [128, 2, 4, 2, 4], BF16)
    mT = sb("mT", [128, 2, 32], BF16)
    lgT = sb("lgT", [128, 128])
    pvs = sb("pvs", [128, 8, T])
    rb = sb("rb", [128, 2, T])
    sc = sb("sc", [128, 2, 16])
    scr = sb("scr", [128, 2, 16])
    z = sb("z", [128, 4, C])
    x1 = [sb(f"x1_{i}", [128, 4, C]) for i in range(2)]
    x1T = sb("x1T", [128, 2, T])
    st = sb("st", [128, 2, 4, 6])
    mv = sb("mv", [128, 2, 4, 2])
    ve = sb("ve", [128, 2, 4])
    rs = sb("rs", [128, 2, 4])
    half = sb("half", [128, 2, 32])
    rr = sb("rr", [128, 12, 4, E])
    rm = sb("rm", [128, 4, 4])
    wkey = sb("wkey", [128, 4, E])
    cT = sb("cT", [E, T])
    th = sb("th", [128, T])
    cf = sb("cf", [128, 2, T])
    zb = sb("zb", [128, T])
    hs = [sb(f"hs{i}", [128, T]) for i in range(2)]

    pS = [ps(f"pS{i}", [128, T]) for i in range(2)]
    pT = [ps(f"pT{i}", [128, T]) for i in range(2)]
    pV = ps("pV", [128, T])
    pG = ps("pG", [128, T])
    pD = [ps(f"pD{i}", [128, 2, C]) for i in range(2)]

    d_part = [dr(f"d_part{i}", [2, 3, H, D, T], BF16) for i in range(2)]
    d_bias = dr("d_bias", [2, 3, 3, H, T], BF16)
    d_m = dr("d_m", [2, 4, 4, 2, 4, 32], BF16)
    d_sum = [dr(f"d_sum{i}", [4, T], F32) for i in range(2)]
    d_comb = dr("d_comb", [E, T], F32)
    d_rec = [dr(f"d_rec{i}", [4, T], F32) for i in range(2)]

    l_qkv = dma(wqkv[:, :, :], A["qkv_wT"].rearrange("(c p) n -> p c n", p=128), s="l_qkv")

    def load_xT(b, *w):
        return dma(xT[:, :, :], A["xT"].rearrange("(c p) n -> p c n", p=128)[:, :, b * T:(b + 1) * T], *w, s="l_xT")

    def load_x(b, *w):
        return dma(z[:, :, :], A["x"][b].rearrange("(t p) c -> p t c", p=128), *w, s="l_x")

    xT_in = load_xT(0)
    dma(rope[:, 0, :], A["k_cos"], s="l_rope")
    l_rope = dma(rope[:, 1, :], A["k_sin"], s="l_rope")
    dma(sl[:, :], A["slopes"].rearrange("(a h) -> a h", a=1).broadcast_to([128, H]), s="l_sl", by="scalar")
    l_sl = dma(tri[:, :, :], A["k_tri"], s="l_sl", by="scalar")
    pos = ee[:, 0, 0, 0:384]
    hot = ee[:, 0, 1, 0:H]
    slc = sb("slc", [128, 1])
    dma(hot, A["k_hot"], s="l_pos", by="scalar")
    l_pos = dma(pos, A["k_pos"], s="l_pos", by="scalar")
    l_ind = []
    for i in range(3):
        for t_, n_, r_ in ((qa[i][96:105, :, :], "k_qind", 9), (ka[i][105:116, :, :], "k_kind", 11)):
            l_ind.append(dma(t_, A[n_].rearrange("r (a t) -> r a t", a=1).broadcast_to([r_, 8, T]),
                             s="l_ind", by="scalar"))
    l_id = None
    l_id = dma(idf[:, :], A["k_idf"], s="l_id")
    x_in = load_x(0)
    dma(wp[:, :, :], A["wp"], s="l_w")
    dma(w1[:, :, :, :], A["w1"], s="l_w")
    dma(w2[:, :, :], A["w2"], s="l_w")
    dma(rw[:, :, :], A["rwT"], s="l_w")
    dma(b1[:, :], A["b1"], s="l_w")
    dma(sb2[:, :], A["sb2"].rearrange("(a c) -> a c", a=1).broadcast_to([128, C]), s="l_w")
    for t in range(4):
        dma(ebb[:, t, :], A["eb"].rearrange("(a c) -> a c", a=1).broadcast_to([128, E]), s="l_w")
    dma(rb2[:, :], A["rb2"], s="l_w")
    l_w = dma(wkey[:, :, :], A["k_key"], s="l_w")

    def link(fn, *w):
        return dve(fn, *w, s="s_link")

    ones = [dve(lambda e, i=i: e.memset(vv[i][:, :, :, 16:32], 1.0), s="s_set") for i in range(2)][-1]
    k = link(lambda e: e.tensor_scalar(slp[:, 0, :], sl[:, :], -32.0, None, ALU.mult), l_sl)
    k = link(lambda e: e.tensor_scalar(slq[:, 0, :], slp[:, 0, :], 65504.0, -65504.0, ALU.min, ALU.max), k)
    k = link(lambda e: e.tensor_tensor(slp[:, 1, :], slp[:, 0, :], slq[:, 0, :], ALU.subtract), k)
    k = link(lambda e: e.tensor_scalar(slq[:, 1, :], slp[:, 1, :], 65504.0, -65504.0, ALU.min, ALU.max), k)

    def spread(dst, m, p):
        v = tri[:, m, :].rearrange("p (a j) -> p a j", a=1).broadcast_to([128, H, 128])
        c = slq[:, p, :].rearrange("p (h a) -> p h a", a=1).broadcast_to([128, H, 128])
        return dve(lambda e: e.tensor_tensor(dst, v, c, ALU.mult), k, s="s_set")

    spread(mB[:, :, :], 0, 0)
    for p in range(2):
        spread(mA[:, p, :, :], 1, p)
    pv_ = ee[:, 1, 0, 0:384]
    pb = parts[0]
    g0 = link(lambda e: e.tensor_tensor(hot, sl[:, :], hot, ALU.mult), l_pos, l_sl)
    g0 = link(lambda e: e.tensor_reduce(slc[:, :], hot, AX, ALU.add), g0)
    g0 = link(lambda e: e.tensor_scalar(pv_, pos, slc[:, 0:1], 32.0, ALU.mult, ALU.mult), g0)
    g1 = link(lambda e: e.tensor_copy(pb[:, 0, 0:384], pv_), g0)
    g2 = link(lambda e: e.tensor_tensor(pv_, pv_, pb[:, 0, 0:384], ALU.subtract), g1)
    g3 = link(lambda e: e.tensor_copy(pb[:, 1, 0:384], pv_), g2)
    g4 = link(lambda e: e.tensor_tensor(pb[:, 2, 0:384], pv_, pb[:, 1, 0:384], ALU.subtract), g3)
    b_w = None
    for p in range(3):
        for side in range(2):
            for r in range(3):
                b_w = dma(d_bias[side, r, p].rearrange("h (c e) -> (h c) e", c=8),
                          pb[:, p, (side * 3 + r) * 64:(side * 3 + r + 1) * 64], g4, s="b_w")
    l_bias = None

    def bias_rows(k_, *w):
        hs_ = slice((k_ % 2) * 8, (k_ % 2) * 8 + 8)
        dma(ka[k_ % 3][96:105, :, :], d_bias[0].rearrange("r p h t -> (r p) h t")[:, hs_, :], b_w, *w,
            s=f"qk_in{k_ % 3}")
        return dma(qa[k_ % 3][105:114, :, :], d_bias[1].rearrange("r p h t -> (r p) h t")[:, hs_, :], b_w, *w,
                   s=f"qk_in{k_ % 3}")

    dve(lambda e: e.memset(half[:, 0, :], -0.5), s="s_set")
    s_half = dve(lambda e: e.memset(half[:, 1, :], 0.5), s="s_set")
    def weights():
        s_w.append(link(lambda e: e.tensor_scalar(rb2[:, :], rb2[:, :], 2.0, None, ALU.mult), l_w))

    s_w = []
    s_const = s_half
    g_free = [None]
    last = {"parts": [b_w, None], "n": 0}
    v_ready = Done()
    st_done = Done()

    SWAP = [(i // 16) * 16 + (i % 16 + 8) % 16 for i in range(32)]

    def qk_tile(b, half_, side, quick=False):
        col = side * 256 + half_ * 128
        for c in range(2):
            yield 854
            t = pe(lambda e, c=c: e.matmul(pG[:, :], wqkv[:, c, col:col + 128], xT[:, c, :], start=(c == 0),
                                           stop=(c == 1)),
                   l_qkv, xT_in_of[b], g_free[0], s="s_g" if c else None)
        i = last["n"] % 2
        last["n"] += 1
        unit = 2 * b + half_
        xT_read(b, t)
        k_ = "quick", i
        if not quick:
            k_ = "usual"
        R_ = ee[:, 2, i, :] if quick else raw[:, :]
        r = act(lambda e: e.copy(R_, pG[:, :]), t, last.get(k_), s="s_raw")
        g_free[0] = r
        later(lambda: qk_rotate(unit, side, i, r, k_))

    def qk_rotate(unit, side, i, r, k_):
        P = parts[i]
        quick = k_ != "usual"
        raw_, sh_ = (ee[:, 2, i, :], ee[:, 2, 2 + i, :]) if quick else (raw[:, :], sh[:, :])
        s_ = dve(lambda e: e.stream_shuffle(sh_, raw_, SWAP), r, last.get(k_), s="s_sh", cost=620)
        on, sem = (dve, "s_link") if quick else (pool, "s_rope")
        a = on(lambda e: e.tensor_tensor(raw_, raw_, rope[:, 0, :], ALU.mult), s_, l_rope, s=sem)
        c = on(lambda e: e.tensor_tensor(sh_, sh_, rope[:, 1, :], ALU.mult), s_, s=sem)
        on(lambda e: e.tensor_tensor(P[:, 0, :], raw_, sh_, ALU.add), a, c, last["parts"][i], s=sem)
        a = on(lambda e: e.tensor_tensor(raw_, raw_, sh_, ALU.add), c, (sem, q.count[sem]), s=sem)
        a = on(lambda e: e.tensor_tensor(P[:, 1, :], raw_, P[:, 0, :], ALU.subtract), a, s=sem)
        a = on(lambda e: e.tensor_tensor(raw_, raw_, P[:, 0, :], ALU.subtract), a, s=sem)
        a = on(lambda e: e.tensor_tensor(P[:, 2, :], raw_, P[:, 1, :], ALU.subtract), a, s=sem)
        last[k_] = a
        if quick:
            quick_done.append(a)
        later(lambda: parts_out(unit, side, i, a), 3 if quick else 7)

    quick_done = []

    def parts_out(unit, side, i, a):
        b, half_ = unit // 2, unit % 2
        P = parts[i]
        hs_ = slice(half_ * 8, half_ * 8 + 8)
        for p in range(3):
            w = dma(d_part[b % 2][side, p, hs_].rearrange("h d t -> (h d) t"), P[:, p, :], a, qk_in.get(unit - 4),
                    s=f"p_w{i}")
        last["parts"][i] = w
        part_in[unit, side] = w

    def assemble(unit):
        free = st_done.get(unit - 3)
        bias_rows(unit, free)
        hs_ = slice((unit % 2) * 8, (unit % 2) * 8 + 8)
        for side in range(2):
            dst = (qa, ka)[side][unit % 3]
            for n, p in enumerate((QPART, KPART)[side]):
                qk_in[unit] = dma(dst[16 * n:16 * n + 16, :, :],
                                  d_part[unit // 2 % 2][side, p, hs_].rearrange("h d t -> d h t"),
                                  part_in[unit, side], free, s=f"qk_in{unit % 3}")

    def v_tiles(b, j):
        for t in range(2):
            for c in range(2):
                yield 427
                tk = pe(lambda e, c=c, t=t: e.matmul(pG[:, t * C:(t + 1) * C],
                                                     xT[:, c, (2 * j + t) * 128:(2 * j + t + 1) * 128],
                                                     wqkv[:, c, 512:768], start=(c == 0), stop=(c == 1)),
                        xT_in_of[b], g_free[0], s="s_g" if (t and c) else None)
        r = act(lambda e: e.copy(vv[b % 2][:, 2 * j:2 * j + 2, :, 0:16],
                                 pG[:, :].rearrange("p (k h d) -> p k h d", k=2, h=H)),
                tk, pv_done.get(4 * (b - 2) + 3), ones, s="s_v")
        g_free[0] = r
        v_ready[b] = r
        xT_read(b, tk)

    xT_left = [6] * NB

    def xT_read(b, tk):
        xT_left[b] -= 1
        if xT_left[b] == 0 and b + 1 < NB:
            xT_in_of[b + 1] = load_xT(b + 1, tk)

    xT_in_of = Done({0: xT_in})
    qk_in, part_in = Done(), Done()
    pv_done = Done()
    xr_in = Done({0: x_in})

    s_max, s_exp, s_ev = Done(), Done(), Done()
    m_in = Done()

    def s_tile(s):
        b, h, t = s // 64, (s // 4) % 16, s % 4
        unit, hu = s // 32, h % 8
        bank = pS[s % 2]
        qs = slice(t * 128, t * 128 + 128)
        pe(lambda e: e.matmul(bank[:, :], qa[unit % 3][0:114, hu, qs], ka[unit % 3][0:114, hu, :], start=True, stop=False),
           qk_in[unit], l_ind[-1], s_max.get(s - 2))
        tk = pe(lambda e: e.matmul(bank[:, qs], tri[:, 1, :], mB[:, h, :], start=False, stop=True), s_const,
                s="s_s")
        g, j = s // 16, (s // 4) % 4
        s_max[s] = dve(lambda e: e.tensor_reduce(negm[:, g % 2, j, t:t + 1], bank[:, :], AX, ALU.max, negate=True),
                       tk, m_split.get(g - 2), s="s_max", cost=640)
        if s % 16 == 15:
            later(lambda: m_rows(g))

    m_split, m_turned, m_out = Done(), Done(), Done()

    def m_rows(g):
        i = g % 2
        a = dve(lambda e: e.tensor_copy(mp[:, i, :, 0, :], negm[:, i, :, :]), s_max[16 * g + 15],
                m_turned.get(g - 2), s="s_mp")
        a = m_split[g] = dve(lambda e: e.tensor_tensor(mp[:, i, :, 1, :], negm[:, i, :, :], mp[:, i, :, 0, :],
                                                       ALU.subtract), a, s="s_mp")
        a = m_turned[g] = dve(lambda e: e.transpose(mT[:, i, :], mp[:, i, :, :, :].rearrange("p h a t -> p (h a t)")),
                              a, m_out.get(g - 2), s="s_mT")
        w = dma(d_m[i].rearrange("a h p t i -> (a h p t) i"), mT[:, i, :], a, m_in.get(g - 2), s=f"m_w{i}")
        m_out[g] = w
        later(lambda: m_rows_in(g, w), 2)

    def m_rows_in(g, w):
        i = g % 2
        u, h0 = g // 2, (g % 2) * 4
        for j in range(4):
            m_in[g] = dma(qa[u % 3][114:116, h0 + j, :].rearrange("p (t a i) -> p t a i", t=4, a=4),
                          d_m[i][:, j].rearrange("a p t i -> p t a i"), w, st_done.get(u - 3), s=f"m_in{i}")

    def st_tile(u):
        g, kt, hh = u // 16, (u % 16) // 4, u % 4
        b, h = g // 4, (g % 4) * 4 + hh
        unit, hu = u // 32, h % 8
        bank = pT[u % 2]
        ks = slice(kt * 128, kt * 128 + 128)
        pe(lambda e: e.matmul(bank[:, :], ka[unit % 3][0:ROWS, hu, ks], qa[unit % 3][0:ROWS, hu, :], start=True, stop=False),
           m_in[g], s_exp.get(u - 2))
        for p in range(2):
            tk = pe(lambda e, p=p: e.matmul(bank[:, ks], tri[:, 0, :], mA[:, p, h, :], start=False, stop=(p == 1)),
                    s="s_t" if p else None)
        if u % 32 == 31:
            st_done[unit] = tk
        w = u // 4
        s_exp[u] = act(lambda e: e.activation(ee[:, w % 3, hh, :], bank[:, :], ACT.Exp, scale=0.25), tk,
                       pv_quad.get(w - 3), g4, *(quick_done if u < 12 else ()), s="s_exp")

    pv_quad = Done()
    rec_done = Done()
    att_done = Done()

    def pv_step(w):
        g, kt = w // 4, w % 4
        b = g // 4
        for hh in range(4):
            h = (g % 4) * 4 + hh
            tk = pe(lambda e, hh=hh, h=h: e.matmul(pV[32 * hh:32 * hh + 32, :], vv[b % 2][:, kt, h, :],
                                                   ee[:, w % 3, hh, :], start=(kt == 0), stop=(kt == 3)),
                    s_exp[4 * w + 3], v_ready[b], s_ev.get(g - 1), s="s_pv" if hh == 3 else None)
        pv_quad[w] = tk
        if kt == 3:
            pv_done[g] = tk
            s_ev[g] = act(lambda e: e.copy(pvs[:, g % 8, :], pV[:, :]), tk, proj_done.get(b - 2), s="s_ev")
            sums_out(g)

    proj_done = Done()

    def sums_out(g):
        i = g % 2
        a = dma(d_sum[i][:, :], pvs[16:128:32, g % 8, :], s_ev[g], sum_in.get(g - 2), s=f"sum_w{i}")
        later(lambda: sums_in(g, a), 2)

    def sums_in(g, a):
        i = g % 2
        sum_in[g] = dma(sc[:, i, :], d_sum[i].rearrange("k (c e) -> (k c) e", e=16), a, rec.get(g - 2),
                        s=f"sum_in{i}")
        later(lambda: reciprocals(g), 3)

    sum_in, rec, rec_w = Done(), Done(), Done()

    def reciprocals(g):
        i = g % 2
        a = rec[g] = dve(lambda e: e.reciprocal(scr[:, i, :], sc[:, i, :]), sum_in[g], rec_w.get(g - 2), s="s_rec")
        a = rec_w[g] = dma(d_rec[i].rearrange("k (c e) -> (k c) e", e=16), scr[:, i, :], a, rec_done.get(g - 2),
                           s=f"rec_w{i}")
        later(lambda: reciprocals_in(g, a), 2)

    def reciprocals_in(g, a):
        i = g % 2
        for hh in range(4):
            rec_done[g] = dma(rb[32 * hh:32 * hh + 32, i, :], d_rec[i][hh:hh + 1].broadcast_to([32, T]), a,
                              att_done.get(g - 2), s=f"rec_in{i}")
        later(lambda: scale_att(g), 3)

    def scale_att(g):
        i = g % 8
        att_done[g] = dve(lambda e: e.tensor_tensor(pvs[:, i, :], pvs[:, i, :], rb[:, g % 2, :], ALU.mult), rec_done[g],
                          s="s_att", cost=640)
        if g % 4 == 3:
            push(1, proj_job, g // 4, 0)

    z_in = Done()
    out_w = Done()

    def proj_job(b, j):
        for t in range(2):
            for g in range(4):
                yield 427
                tk = pe(lambda e, t=t, g=g: e.matmul(pG[:, t * C:(t + 1) * C],
                                                     pvs[:, 4 * (b % 2) + g,
                                                         (2 * j + t) * 128:(2 * j + t + 1) * 128],
                                                     wp[:, g, :], start=(g == 0), stop=(g == 3)),
                        att_done[4 * b + 3], l_w, g_free[0], s="s_g" if (t and g == 3) else None)
        if j == 1:
            proj_done[b] = tk
        early(lambda: residual(b, j, tk))
        if j == 0:
            push(1, proj_job, b, 1)
        else:
            later(lambda: norm1_stats(b), 2)
            later(lambda: norm1(b), 5)

    def residual(b, j, tk):
        zz = z[:, 2 * j:2 * j + 2, :].rearrange("p t c -> p (t c)")
        z_in[b, j] = dve(lambda e: e.tensor_tensor(zz, pG[:, :], zz, ALU.add), tk, xr_in[b], s="s_z",
                           cost=640)
        g_free[0] = z_in[b, j]
        for t in (2 * j, 2 * j + 1):
            stats[b, 0, t] = dve(lambda e, t=t: e.bn_stats(st[:, 0, t, :], z[:, t, :]), z_in[b, j], s="s_st", cost=350)

    stats = Done()

    def rstd(b, k):
        a = None
        for t in range(4):
            a = dve(lambda e, t=t: e.bn_aggr(mv[:, k, t, :], st[:, k, t, :]), stats[b, k, t], s="s_st", cost=350)
        a = link(lambda e: e.tensor_scalar(ve[:, k, :], mv[:, k, :, 1], EPS, None, ALU.add), a)
        return pool(lambda e: e.tensor_tensor(rs[:, k, :], ve[:, k, :], half[:, 0, 0:4], ALU.pow), a, s_half,
                    s="s_pow")

    def norm1_stats(b):
        x1_rs[b] = rstd(b, 0)

    def norm1(b):
        if b > 1 and b - 2 not in out_w:
            return later(lambda: norm1(b))
        a = x1_rs[b]
        for t in range(4):
            n = dve(lambda e, t=t: e.tensor_scalar(x1[b % 2][:, t, :], z[:, t, :], mv[:, 0, t, 0:1], rs[:, 0, t:t + 1],
                                                   ALU.subtract, ALU.mult), a, out_w.get(b - 2), s="s_x1", cost=200)
        x1_in[b] = n
        if b + 1 < NB:
            xr_in[b + 1] = load_x(b + 1, n)
        push(2, turn_job, b, 0)

    x1_rs, x1_in, x1T_in, ffn_read = Done(), Done(), Done(), Done()

    def turn_job(b, c):
        for t in range(4):
            yield 178
            tk = pe(lambda e, t=t: e.transpose(pG[:, t * 128:t * 128 + 128], x1[b % 2][:, t, c * 128:c * 128 + 128],
                                               idf[:, :]), x1_in[b], g_free[0], s="s_g" if t == 3 else None)
        r = act(lambda e: e.copy(x1T[:, c, :], pG[:, :]), tk, up_done.get(b - 1), s="s_x1T")
        g_free[0] = r
        x1T_in[b] = r
        if c == 1:
            for t in range(4):
                r = pool(lambda e, t=t: e.tensor_tensor(x1[b % 2][:, t, :], x1[b % 2][:, t, :], sb2[:, :], ALU.add), tk, l_w,
                         s="s_x1b")
            x1b[b] = r
            push(2, route_job, b)
            push(2, up_job, b, 0)
        else:
            push(1, turn_job, b, 1)

    x1b = Done()

    def route_job(b):
        yield 480
        for c in range(2):
            for t in range(4):
                tk = pe(lambda e, t=t, c=c: e.matmul(pG[32 * t:32 * t + 32, 0:128], rw[:, c, :],
                                                     x1T[:, c, t * 128:t * 128 + 128], start=(c == 0), stop=(c == 1)),
                        x1T_in[b], g_free[0], s="s_g" if (t == 3 and c) else None)
        push(2, route_turn, b)
        g_free[0] = lg_in[b] = act(lambda e: e.copy(lgT[:, :], pG[:, 0:128]), tk, lg_read.get(b - 1), s="s_lgT")

    def route_turn(b):
        yield 180
        tk = pe(lambda e: e.transpose(pG[:, 0:128], lgT[:, :], idf[:, :]), lg_in[b], g_free[0], s="s_g")
        lg_read[b] = tk
        early(lambda: route_logits(b, tk))
        later(lambda: route_softplus(b), 2)

    def route_logits(b, tk):
        a = link(lambda e: e.tensor_tensor(R(0), pG[:, 0:128].rearrange("p (t e) -> p t e", t=4)[:, :, 0:E],
                                           ebb[:, :, :], ALU.add), tk, cp_read.get(b - 1))
        g_free[0] = a
        a = link(lambda e: e.tensor_scalar(R(1), R(0), -1.0, None, ALU.mult), a)
        a = link(lambda e: e.tensor_tensor(R(2), R(0), R(1), ALU.min), a)
        a = act(lambda e: e.activation(R(3), R(2), ACT.Exp), a, s="s_u")
        route_u[b] = a

    lg_in, lg_read = Done(), Done()

    def R(i):
        return rr[:, i, :, :]

    def RB(i):
        return rm[:, i, :].rearrange("p (t a) -> p t a", a=1).broadcast_to([128, 4, E])

    route_u, cp_read, route_a, route_c = Done(), Done(), Done(), Done()

    def route_softplus(b):
        todo = [lambda e: e.tensor_scalar(R(1), R(3), 2.0, None, ALU.add),
                lambda e: e.reciprocal(R(2), R(1)),
                lambda e: e.tensor_tensor(R(4), R(3), R(2), ALU.mult),
                lambda e: e.tensor_tensor(R(5), R(4), R(4), ALU.mult),
                lambda e: e.tensor_scalar(R(6), R(5), 1.0 / 17, None, ALU.mult)]
        todo += [lambda e, n=n: e.scalar_tensor_tensor(R(6), R(6), 1.0 / n, R(5), ALU.add, ALU.mult)
                 for n in (15, 13, 11, 9, 7, 5, 3)]
        todo += [lambda e: e.scalar_tensor_tensor(R(6), R(6), 1.0, R(4), ALU.add, ALU.mult),
                 lambda e: e.tensor_scalar(R(1), R(0), 0.0, None, ALU.max),
                 lambda e: e.scalar_tensor_tensor(R(6), R(6), 2.0, R(1), ALU.mult, ALU.add)]

        def done(a):
            route_a[b] = pool(lambda e: e.tensor_tensor(R(7).rearrange("p t e -> p (t e)"),
                                                        R(6).rearrange("p t e -> p (t e)"), half[:, 1, :], ALU.pow),
                              a, s="s_pow")
            later(lambda: route_top2(b), TOP)

        chain(todo, route_u[b], done)

    def chain(todo, a, done):
        for fn in todo[:LINKS]:
            a = link(fn, a)
        if todo[LINKS:]:
            later(lambda: chain(todo[LINKS:], a, done))
        else:
            done(a)

    def route_top2(b):
        todo = []
        for n, src in ((0, 7), (1, 11)):
            todo += [lambda e, src=src: e.tensor_reduce(rm[:, 0, :], R(src), AX, ALU.max),
                     lambda e, src=src: e.tensor_tensor(R(1), R(src), RB(0), ALU.is_equal),
                     lambda e: e.tensor_tensor(R(2), R(1), wkey[:, :, :], ALU.mult),
                     lambda e: e.tensor_reduce(rm[:, 1, :], R(2), AX, ALU.max),
                     lambda e, n=n: e.tensor_tensor(R(8 + n), R(2), RB(1), ALU.is_equal)]
            if n == 0:
                todo.append(lambda e: e.scalar_tensor_tensor(R(11), R(8), -1e30, R(7), ALU.mult, ALU.add))
        todo += [lambda e: e.tensor_tensor(R(10), R(8), R(9), ALU.add),
                 lambda e: e.scalar_tensor_tensor(R(10), R(10), 0.5, R(7), ALU.mult, ALU.mult)]

        def done(a):
            route_c[b] = a
            push(1, cT_job, b)

        chain(todo, route_a[b], done)

    cT_in = Done()

    def cT_job(b):
        for t in range(4):
            yield 178
            tk = pe(lambda e, t=t: e.transpose(pG[0:E, t * 128:t * 128 + 128], R(10)[:, t, :], idf[:, :]),
                    route_c[b], g_free[0], s="s_g" if t == 3 else None)
        cp_read[b] = tk
        r = act(lambda e: e.copy(cT[:, :], pG[0:E, 0:T]), tk, ffn_read.get(b - 1), s="s_cT")
        g_free[0] = r
        w = dma(d_comb, cT[:, :], r, s="comb_w")
        later(lambda: (cf_load(b, 1, w), cf_load(b, 2, w)), 2)
        comb_w[b] = w
        push(4, up_job, b, 1)

    def cf_load(b, e_, w):
        n = 9 * b + e_
        cf_in[n] = dma(cf[:, e_ % 2, :], d_comb[e_ - 1:e_].broadcast_to([128, T]), w, a_done.get(n - 2 if e_ > 2 else n - 3),
                       s=f"cf_in{e_ % 2}")

    up_done, th_in = Done(), Done()
    a_done, comb_w, cf_in, hs_in, down = Done(), Done(), Done(), Done(), Done()

    def up_job(b, e_):
        n = 9 * b + e_
        for c in range(2):
            yield 854
            tk = pe(lambda e, c=c: e.matmul(pG[:, :], w1[:, e_, c, :], x1T[:, c, :], start=(c == 0), stop=(c == 1)),
                    x1T_in[b], l_w, g_free[0], s="s_g" if c else None)
        a = act(lambda e: e.activation(zb[:, :], pG[:, :], ACT.Identity, bias=b1[:, e_:e_ + 1]), tk, l_w,
                a_done.get(n - 1), th_in.get(n - 1), s="s_zb")
        g_free[0] = a
        r = act(lambda e: e.activation(th[:, :], zb[:, :], ACT.Tanh, scale=0.5), a, hs_in.get(n - 1), s="s_th")
        th_in[n] = r
        later(lambda: gate(b, e_, a, r))
        push(DOWN, down_job, b, e_)
        if 0 < e_ < 8:
            push(1, up_job, b, e_ + 1)
        if e_ == 8:
            up_done[b] = tk

    def gate(b, e_, a, r):
        n = 9 * b + e_
        h_ = hs[n % 2]
        if e_ == 0:
            a = dve(lambda e: e.tensor_scalar(h_[:, :], zb[:, :], 0.5, None, ALU.mult), a, down.get(n - 2),
                    s="s_a", cost=350)
        else:
            a = dve(lambda e: e.tensor_tensor(h_[:, :], zb[:, :], cf[:, e_ % 2, :], ALU.mult), a, cf_in[n],
                    down.get(n - 2), s="s_a", cost=600)
        a_done[n] = a
        if 0 < e_ < 7:
            later(lambda: cf_load(b, e_ + 2, comb_w[b]))
        hs_in[n] = dve(lambda e: e.scalar_tensor_tensor(h_[:, :], th[:, :], 1.0, h_[:, :], ALU.add, ALU.mult),
                       a, r, s="s_hs", cost=620)

    z2_in = Done()

    def down_job(b, e_):
        n = 9 * b + e_
        for t in range(4):
            yield 427
            tk = pe(lambda e, t=t: e.matmul(pD[t // 2][:, t % 2, :], hs[n % 2][:, t * 128:t * 128 + 128],
                                            w2[:, e_, :], start=(e_ == 0 and t % 2 == 0), stop=False,
                                            skip_group_check=True),
                    hs_in[n], z2_in.get(b - 1), s="s_d" if t == 3 else None)
        down[n] = tk
        if e_ == 8:
            for t in range(4):
                yield 427
                tk = pe(lambda e, t=t: e.matmul(pD[t // 2][:, t % 2, :], cT[:, t * 128:t * 128 + 128], rb2[:, :],
                                                start=False, stop=True, skip_group_check=True),
                        s_w[0], s="s_d" if t == 3 else None)
            ffn_read[b] = tk
            early(lambda: residual2(b, tk))
            later(lambda: norm2_stats(b), 2)
            later(lambda: norm2(b), 5)

    def residual2(b, tk):
        for j in range(2):
            xx = x1[b % 2][:, 2 * j:2 * j + 2, :].rearrange("p t c -> p (t c)")
            z2_in[b] = dve(lambda e, j=j, xx=xx: e.tensor_tensor(
                xx, pD[j][:, :, :].rearrange("p t c -> p (t c)"), xx, ALU.add), tk, x1b[b], s="s_z2", cost=640)
            for t in (2 * j, 2 * j + 1):
                stats[b, 1, t] = dve(lambda e, t=t: e.bn_stats(st[:, 1, t, :], x1[b % 2][:, t, :]), z2_in[b], s="s_st", cost=350)

    def norm2_stats(b):
        x2_rs[b] = rstd(b, 1)

    x2_rs = Done()

    def norm2(b):
        a = x2_rs[b]
        for t in range(4):
            n = dve(lambda e, t=t: e.tensor_scalar(x1[b % 2][:, t, :], x1[b % 2][:, t, :], mv[:, 1, t, 0:1], rs[:, 1, t:t + 1],
                                                   ALU.subtract, ALU.mult), a, s="s_o", cost=200)
        out_w[b] = dma(out[b].rearrange("(t p) c -> p t c", p=128), x1[b % 2][:, :, :], n, s="out_w")

    slot, clock, number = [-1], [0], [0]
    first, soon, ready, running = [], [], [], []
    g_from, qk_from = [0], [0]

    def early(fn):
        first.append(fn)

    def later(fn, n=1):
        soon.append((slot[0] + 1, clock[0] + (n - 1) * STEP, fn))

    def push(n, fn, *a, from_slot=0):
        number[0] += 1
        ready.append((max(slot[0] + 1, from_slot), clock[0] + (n - 1) * STEP, number[0], fn, a))

    def rank(j):
        if j[3] == down_job:
            return (0, j[2])
        return (2 if j[3] in (qk_tile, v_tiles) and slot[0] < j[0] + URGENT else 1, j[2])

    def pick():
        for j in sorted(ready, key=rank):
            if j[3] == proj_job and j[4][0] not in xr_in or j[3] in (qk_tile, v_tiles) and j[4][0] not in xT_in_of:
                continue
            if j[0] <= slot[0] and j[1] <= clock[0] and (j[3] != qk_tile or j[4][-1] or qk_from[0] <= clock[0]) \
                    and (j[3] == down_job or g_from[0] <= slot[0]):
                ready.remove(j)
                return j[3], j[3](*j[4])
        return None

    def spend(budget):
        while budget > 0:
            if not running:
                j = pick()
                if j is None:
                    return min(budget, 0)
                running.extend(j + (next(j[1]),))
            fn, job, cost = running
            budget -= cost
            clock[0] += cost
            try:
                running[2] = next(job)
            except StopIteration:
                running.clear()
                if fn != down_job:
                    g_from[0] = slot[0] + 1
                    if fn == qk_tile:
                        qk_from[0] = clock[0] + QK_GAP
        return budget

    def turn():
        slot[0] += 1
        while first:
            first.pop(0)()

    def settle():
        due = [j for j in soon if j[0] <= slot[0] and j[1] <= clock[0]]
        for j in due:
            soon.remove(j)
        for j in due:
            j[2]()

    for side in range(2):
        push(1, qk_tile, 0, 0, side, True)
    while ready or running or soon:
        turn()
        settle()
        spend(1e9)
        clock[0] += STEP
    assemble(0)
    for side in range(2):
        push(1, qk_tile, 0, 1, side, True)
    for j in range(2):
        push(1, v_tiles, 0, j)
    later(weights)
    base = slot[0] + 1
    wants = {20: lambda: assemble(1)}
    for b in range(NB - 1):
        wants[64 * b + 54] = lambda b=b: assemble(2 * b + 2)
        wants[64 * b + 62] = lambda b=b: assemble(2 * b + 3)
    for b in range(NB - 1):
        for n in range(4):
            push(1, qk_tile, b + 1, n // 2, n % 2, False, from_slot=base + (64 * b + QK_AT if b else 4))
        for j in range(2):
            push(1, v_tiles, b + 1, j, from_slot=base + 64 * b + V_AT)
    ready.sort()
    credit, s = 0, -1
    while s < NTILE or ready or running or soon or first:
        s += 1
        turn()
        start = clock[0]
        load.update(vector=0, scalar=0)
        if s < NTILE:
            s_tile(s)
            clock[0] += 290
        if 0 <= s - LAG < NTILE:
            st_tile(s - LAG)
            clock[0] += 340
        settle()
        if s in wants:
            wants[s]()
        v = s - LAG - PVLAG
        credit = min(credit, RATE) + RATE
        if v >= 0 and v % 4 == 0 and v // 4 < NTILE // 4:
            pv_step(v // 4)
            credit -= 930
            clock[0] += 930
        if s >= NTILE + LAG:
            credit = 3000
        credit = spend(credit)
        clock[0] = max(clock[0], start + max(700, 1.06 * max(load.values())))
    q.put("sync", None, (out_w[NB - 1],))

    block = ctx.enter_context(nc.Block())

    @block.sync
    def _(e):
        q.run("sync", e)

    @block.tensor
    def _(e):
        q.run("tensor", e)

    @block.vector
    def _(e):
        q.run("vector", e)

    @block.scalar
    def _(e):
        q.run("scalar", e)

    @block.gpsimd
    def _(e):
        q.run("gpsimd", e)


def tables():
    bf = mybir.dt.np(BF16)
    f = np.float32
    t = {}
    inv = (f(1.0) / (f(10000.0) ** (np.arange(0, D, 2, dtype=f) / f(D)))).astype(f)
    fr = (np.arange(T, dtype=f)[:, None] * inv[None, :]).astype(f)
    row = np.arange(128) % D
    t["k_cos"] = np.ascontiguousarray(np.cos(fr).astype(f)[:, row % 8].T)
    sign = np.where(row < 8, f(-1), f(1))[:, None]
    t["k_sin"] = np.ascontiguousarray(np.sin(fr).astype(f)[:, row % 8].T * sign)
    j = np.arange(128)
    t["k_hot"] = (np.arange(128)[:, None] // 8 == np.arange(H)[None, :]).astype(f)
    t["k_tri"] = np.stack([(j[None, :] <= j[:, None]), (j[:, None] < j[None, :])], 1).astype(bf)
    x = np.arange(T)
    kv = np.stack([(x - 128 * (r + 1)) * (x // 128 == r) for r in range(3)])
    qv = np.stack([-(x - 128 * (r + 1)) * (x // 128 > r) for r in range(3)])
    pos = np.stack([kv, qv]).reshape(6, 8, 64).transpose(1, 0, 2).reshape(8, 384)
    t["k_pos"] = np.tile(pos, (16, 1)).astype(f)
    t["k_qind"] = np.repeat(np.stack([x // 128 > r for r in range(3)]), 3, 0).astype(bf)
    t["k_kind"] = np.concatenate([np.repeat(np.stack([x // 128 == r for r in range(3)]), 3, 0),
                                  np.ones((2, T), bool)]).astype(bf)
    t["k_idf"] = np.eye(128, dtype=f)
    t["k_key"] = np.broadcast_to((8 - np.arange(E)).astype(f), (128, 4, E)).copy()
    return t


def kernel(**inputs):
    import concourse.bacc as _bacc
    from concourse.bass_utils import run_bass_kernel_spmd as _run

    i = {n: np.asarray(a) for n, a in inputs.items()}
    x = i["L0_attn_x"]
    a = {"x": x, "xT": x.reshape(NB * T, C).T, "qkv_wT": i["L0_attn_qkv_w"].T, "slopes": i["L0_attn_slopes"]}
    wp = np.zeros((4, 4, 32, C), np.float32)
    wp[:, :, 0:16, :] = i["L0_attn_proj_w"].T.reshape(4, 4, 16, C)
    wp[0, 0, 16, :] = i["L0_attn_proj_b"]
    a["wp"] = wp.transpose(1, 2, 0, 3).reshape(128, 4, C)
    w1 = np.concatenate([i["L0_ffn_sW1"][None], i["L0_ffn_rW1"]])
    a["w1"] = w1.reshape(9, 2, 128, 128).transpose(2, 0, 1, 3)
    a["w2"] = np.concatenate([i["L0_ffn_sW2"][None], i["L0_ffn_rW2"]]).transpose(1, 0, 2)
    a["b1"] = np.concatenate([i["L0_ffn_sb1"][None], i["L0_ffn_rb1"]]).T
    rw = np.zeros((128, 2, 32), np.float32)
    rw[:, :, 0:E] = i["L0_ffn_routing_W"].T.reshape(2, 128, E).transpose(1, 0, 2)
    a["rwT"] = rw
    a["eb"] = i["L0_ffn_expert_bias"]
    a["sb2"] = i["L0_ffn_sb2"]
    a["rb2"] = i["L0_ffn_rb2"]
    a.update(tables())
    nc = _bacc.Bacc("TRN2", target_bir_lowering=False, num_devices=1)
    arrays, aps = {}, {}
    for n, v in a.items():
        v = np.ascontiguousarray(v)
        arrays["in_" + n] = v
        aps[n] = nc.dram_tensor("in_" + n, v.shape, mybir.dt.from_np(v.dtype), kind="ExternalInput").ap()
    out = nc.dram_tensor("out_0", (NB, T, C), F32, kind="ExternalOutput").ap()
    build(nc, aps, out)
    r = _run(nc, [arrays], core_ids=[0])
    return r.results[0]["out_0"]
```

```python
from contextlib import ExitStack

import numpy as np
import concourse.bass as bass
from concourse import mybir

ALU = mybir.AluOpType
ACT = mybir.ActivationFunctionType
F32 = mybir.dt.float32
BF16 = mybir.dt.bfloat16
F16 = mybir.dt.float16
F32R = mybir.dt.float32r
AX = mybir.AxisListType.X

NB, T, C = 16, 512, 256
H, D = 16, 16
E = 8
LAG = 29
PVLAG = 5
NTILE = NB * 64
ROWS = 116
EPS = 1e-5
RATE = 1404
FAST = 1500
URGENT = 41
AHEAD = 2246
SLACK = 180
LINKS = 6
SHARE = 1539
QK_AT = -5
V_AT = 49
LATENCY = 225
QPART = (0, 0, 1, 1, 0, 2)
KPART = (0, 1, 0, 1, 2, 0)


class Done(dict):

    def get(self, k):
        return None if k < 0 else self[k]


class Queues:

    def __init__(self, nc, ctx):
        self.nc, self.ctx = nc, ctx
        self.sems, self.count = {}, {}
        self.todo = {e: [] for e in ("tensor", "vector", "scalar", "gpsimd", "sync")}
        self.free = dict.fromkeys(("tensor", "vector", "scalar", "gpsimd", "sync", "dma"), 0)
        self.time = {}

    def put(self, engine, fn, waits=(), sem=None, inc=1, cost=0):
        if sem is not None and sem not in self.sems:
            self.sems[sem] = self.ctx.enter_context(self.nc.semaphore(sem))
            self.count[sem] = 0
        waits = tuple(w for w in waits if w is not None)
        self.todo[engine].append((waits, fn, sem, inc))
        start = max([self.free[engine]] + [self.time[w] for w in waits])
        if inc == 16:
            self.free[engine] = start
            self.free["dma"] = max(self.free["dma"], start) + 480
            end = self.free["dma"] + 2000
        else:
            end = self.free[engine] = start + cost
        if sem is None:
            return None
        self.count[sem] += inc
        self.time[sem, self.count[sem]] = end + LATENCY
        return (sem, self.count[sem])

    def run(self, engine, eng):
        passed = {}
        for waits, fn, sem, inc in self.todo[engine]:
            for name, value in waits:
                if passed.get(name, 0) < value:
                    eng.wait_ge(self.sems[name], value)
                    passed[name] = value
            if fn is None:
                continue
            ins = fn(eng)
            if sem is not None:
                ins.then_inc(self.sems[sem], inc)


def build(nc, A, out):
    with ExitStack() as ctx:
        _build(nc, ctx, A, out)


def _build(nc, ctx, A, out):
    def sb(name, shape, dt=F32):
        return ctx.enter_context(nc.sbuf_tensor(name, shape, dt))

    def ps(name, shape, dt=F32):
        return ctx.enter_context(nc.psum_tensor(name, shape, dt))

    def dr(name, shape, dt):
        return nc.dram_tensor(name, shape, dt, kind="Internal").ap()

    q = Queues(nc, ctx)

    share = [0]
    piece = [0]

    def pe(fn, *w, s=None):
        cost, piece[0] = piece[0], 0
        return q.put("tensor", fn, w, s, cost=cost)

    def dve(fn, *w, s=None, cost=110):
        share[0] += cost
        return q.put("vector", fn, w, s, cost=cost)

    def act(fn, *w, s=None, cost=500):
        return q.put("scalar", fn, w, s, cost=cost)

    def pool(fn, *w, s=None, cost=700):
        return q.put("gpsimd", fn, w, s, cost=cost)

    def dma(dst, src, *w, s, by="sync"):
        return q.put(by, lambda e: e.dma_start(dst, src), w, s, 16)

    qa = [sb(f"qa{i}", [128, 8, T], BF16) for i in range(3)]
    ka = [sb(f"ka{i}", [128, 8, T], BF16) for i in range(3)]
    ee = sb("ee", [128, 3, 4, T])
    vv = [sb(f"vv{i}", [128, 4, H, 32]) for i in range(2)]
    xT = sb("xT", [128, 2, T])
    wqkv = sb("wqkv", [128, 2, 768])
    wp = sb("wp", [128, 4, C])
    w1 = [sb(f"w1_{i}", [128, 9, 2, 128]) for i in range(2)]
    w2 = sb("w2", [128, 9, C])
    rw = sb("rw", [128, 2, 32])
    b1 = sb("b1", [128, 9])
    ebb = sb("ebb", [128, 4, E])
    sb2 = sb("sb2", [128, C])
    rb2 = sb("rb2", [E, C])
    rope = sb("rope", [128, 2, T])
    raw = sb("raw", [128, T])
    sh = sb("sh", [128, T])
    parts = [sb("parts", [128, 3, T], BF16),
             ee[:, 1, 1:4, :].rearrange("p a t -> p (a t)").bitcast(BF16)[:, 0:3 * T].rearrange("p (a t) -> p a t", a=3)]
    idf = sb("idf", [128, 128])
    tri = sb("tri", [128, 2, 128], BF16)
    mA = sb("mA", [128, 2, H, 128], F16)
    mB = sb("mB", [128, H, 128], F16)
    sl = sb("sl", [128, H])
    slp = sb("slp", [128, 2, H])
    slq = sb("slq", [128, 2, H], F16)
    negm = sb("negm", [128, 2, 4, 4])
    mp = sb("mp", [128, 2, 4, 2, 4], BF16)
    mT = sb("mT", [128, 2, 32], BF16)
    lgT = sb("lgT", [128, 128])
    pvs = sb("pvs", [128, 5, T])
    rb = sb("rb", [128, 2, T])
    sc = sb("sc", [128, 2, 16])
    scr = sb("scr", [128, 2, 16])
    z = sb("z", [128, 4, C])
    x1 = [sb(f"x1_{i}", [128, 4, C]) for i in range(2)]
    x1T = [sb(f"x1T_{i}", [128, 2, T]) for i in range(2)]
    st = sb("st", [128, 2, 4, 6])
    mv = sb("mv", [128, 2, 4, 2])
    ve = sb("ve", [128, 2, 4])
    rs = sb("rs", [128, 2, 4])
    half = sb("half", [128, 2, 32])
    rr = sb("rr", [128, 12, 4, E])
    rm = sb("rm", [128, 4, 4])
    wkey = sb("wkey", [128, 4, E])
    cT = sb("cT", [E, T])
    th = sb("th", [128, T])
    cf = sb("cf", [128, 2, T])
    zb = sb("zb", [128, T])
    hs = [sb(f"hs{i}", [128, T]) for i in range(2)]

    pS = [ps(f"pS{i}", [128, T]) for i in range(2)]
    pT = [ps(f"pT{i}", [128, T]) for i in range(2)]
    pV = ps("pV", [128, T])
    pG = ps("pG", [128, T])
    pD = [ps(f"pD{i}", [128, 2, C]) for i in range(2)]

    d_part = [dr(f"d_part{i}", [2, 3, H, D, T], BF16) for i in range(2)]
    d_bias = dr("d_bias", [2, 3, 3, H, T], BF16)
    d_m = dr("d_m", [2, 4, 4, 2, 4, 32], BF16)
    d_sum = [dr(f"d_sum{i}", [4, T], F32) for i in range(2)]
    d_comb = dr("d_comb", [E, T], F32)
    d_rec = [dr(f"d_rec{i}", [4, T], F32) for i in range(2)]

    l_qkv = dma(wqkv[:, :, :], A["qkv_wT"].rearrange("(c p) n -> p c n", p=128), s="l_qkv")

    def load_xT(b, *w):
        return dma(xT[:, :, :], A["xT"].rearrange("(c p) n -> p c n", p=128)[:, :, b * T:(b + 1) * T], *w, s="l_xT")

    def load_x(b, *w):
        return dma(z[:, :, :], A["x"][b].rearrange("(t p) c -> p t c", p=128), *w, s="l_x")

    xT_in = load_xT(0)
    dma(rope[:, 0, :], A["k_cos"], s="l_rope")
    l_rope = dma(rope[:, 1, :], A["k_sin"], s="l_rope")
    dma(sl[:, :], A["slopes"].rearrange("(a h) -> a h", a=1).broadcast_to([128, H]), s="l_sl", by="scalar")
    l_sl = dma(tri[:, :, :], A["k_tri"], s="l_sl", by="scalar")
    pos = ee[:, 0, 0, 0:384]
    hot = ee[:, 0, 1, 0:H]
    slc = sb("slc", [128, 1])
    dma(hot, A["k_hot"], s="l_pos", by="scalar")
    l_pos = dma(pos, A["k_pos"], s="l_pos", by="scalar")
    l_ind = []
    for i in range(3):
        for t_, n_, r_ in ((qa[i][96:105, :, :], "k_qind", 9), (ka[i][105:116, :, :], "k_kind", 11)):
            l_ind.append(dma(t_, A[n_].rearrange("r (a t) -> r a t", a=1).broadcast_to([r_, 8, T]),
                             s="l_ind", by="scalar"))
    l_id = None
    l_id = dma(idf[:, :], A["k_idf"], s="l_id")
    x_in = load_x(0)
    dma(wp[:, :, :], A["wp"], s="l_w")
    stage = ((x1[0][:, :, :].rearrange("p t c -> p (t c)"), slice(0, 4)),
             (x1[1][:, :, :].rearrange("p t c -> p (t c)"), slice(4, 8)), (th[:, 0:C], slice(8, 9)))
    for t_, e_ in stage:
        dma(t_.rearrange("p (e c n) -> p e c n", c=2, n=128), A["w1"][:, e_], s="l_w")
    dma(w2[:, :, :], A["w2"], s="l_w")
    dma(rw[:, :, :], A["rwT"], s="l_w")
    dma(b1[:, :], A["b1"], s="l_w")
    dma(sb2[:, :], A["sb2"].rearrange("(a c) -> a c", a=1).broadcast_to([128, C]), s="l_w")
    for t in range(4):
        dma(ebb[:, t, :], A["eb"].rearrange("(a c) -> a c", a=1).broadcast_to([128, E]), s="l_w")
    dma(rb2[:, :], A["rb2"], s="l_w")
    l_w = dma(wkey[:, :, :], A["k_key"], s="l_w")

    def link(fn, *w):
        share[0] += 100
        return dve(fn, *w, s="s_link")

    ones = [dve(lambda e, i=i: e.memset(vv[i][:, :, :, 16:32], 1.0), s="s_set") for i in range(2)][-1]
    k = link(lambda e: e.tensor_scalar(slp[:, 0, :], sl[:, :], -32.0, None, ALU.mult), l_sl)
    k = link(lambda e: e.tensor_scalar(slq[:, 0, :], slp[:, 0, :], 65504.0, -65504.0, ALU.min, ALU.max), k)
    k = link(lambda e: e.tensor_tensor(slp[:, 1, :], slp[:, 0, :], slq[:, 0, :], ALU.subtract), k)
    k = link(lambda e: e.tensor_scalar(slq[:, 1, :], slp[:, 1, :], 65504.0, -65504.0, ALU.min, ALU.max), k)

    c_ready = k

    def spread(dst, m, p):
        v = tri[:, m, :].rearrange("p (a j) -> p a j", a=1).broadcast_to([128, H, 128])
        c = slq[:, p, :].rearrange("p (h a) -> p h a", a=1).broadcast_to([128, H, 128])
        return dve(lambda e: e.tensor_tensor(dst, v, c, ALU.mult), c_ready, s="s_set", cost=2200)

    spread(mB[:, :, :], 0, 0)
    pv_ = ee[:, 1, 0, 0:384]
    pb = cf[:, :, :].rearrange("p a t -> p (a t)").bitcast(BF16)[:, 0:1536].rearrange("p (a t) -> p a t", a=3)
    g0 = link(lambda e: e.tensor_tensor(hot, sl[:, :], hot, ALU.mult), l_pos, l_sl)
    g0 = link(lambda e: e.tensor_reduce(slc[:, :], hot, AX, ALU.add), g0)
    g0 = link(lambda e: e.tensor_scalar(pv_, pos, slc[:, 0:1], 32.0, ALU.mult, ALU.mult), g0)
    g1 = link(lambda e: e.tensor_copy(pb[:, 0, 0:384], pv_), g0)
    g2 = link(lambda e: e.tensor_tensor(pv_, pv_, pb[:, 0, 0:384], ALU.subtract), g1)
    g3 = link(lambda e: e.tensor_copy(pb[:, 1, 0:384], pv_), g2)
    g4 = link(lambda e: e.tensor_tensor(pb[:, 2, 0:384], pv_, pb[:, 1, 0:384], ALU.subtract), g3)
    b_w = None
    for p in range(3):
        b_w = dma(d_bias[:, :, p].rearrange("s r h (c e) -> (h c) (s r) e", c=8),
                  pb[:, p, 0:384].rearrange("p (k e) -> p k e", k=6), g4, s="b_w")

    def bias_rows(k_, *w):
        hs_ = slice((k_ % 2) * 8, (k_ % 2) * 8 + 8)
        dma(ka[k_ % 3][96:105, :, :], d_bias[0].rearrange("r p h t -> (r p) h t")[:, hs_, :], b_w, *w,
            s=f"qk_in{k_ % 3}")
        return dma(qa[k_ % 3][105:114, :, :], d_bias[1].rearrange("r p h t -> (r p) h t")[:, hs_, :], b_w, *w,
                   s=f"qk_in{k_ % 3}")

    dve(lambda e: e.memset(half[:, 0, :], -0.5), s="s_set")
    s_half = dve(lambda e: e.memset(half[:, 1, :], 0.5), s="s_set")
    def weights():
        for p in range(2):
            s_mA.append(spread(mA[:, p, :, :], 1, p))
        w1_in = None
        for t_, e_ in stage:
            v = [w[:, e_, :, :].rearrange("p e c n -> p (e c n)") for w in w1]
            k = link(lambda e, t_=t_, v=v: e.tensor_copy(v[0].bitcast(F32R), t_), l_w)
            w1_in = link(lambda e, t_=t_, v=v: e.tensor_tensor(v[1].bitcast(F32R), t_, v[0], ALU.subtract), k)
        s_w1.append(w1_in)
        s_w.append(link(lambda e: e.tensor_scalar(rb2[:, :], rb2[:, :], 2.0, None, ALU.mult), l_w))

    s_w, s_mA, s_w1 = [], [], []
    s_const = s_half
    g_free = [None]
    last = {"parts": [None, None], "n": 0}
    v_ready = Done()
    st_done = Done()

    SWAP = [(i // 16) * 16 + (i % 16 + 8) % 16 for i in range(32)]

    def qk_tile(b, half_, side, quick=0):
        col = side * 256 + half_ * 128
        for c in range(2):
            yield 854
            t = pe(lambda e, c=c: e.matmul(pG[:, :], wqkv[:, c, col:col + 128], xT[:, c, :], start=(c == 0),
                                           stop=(c == 1)),
                   l_qkv, xT_in_of[b], g_free[0], s="s_g" if c else None)
        i = last["n"] % 2
        last["n"] += 1
        unit = 2 * b + half_
        xT_read(b, t)
        k_ = ("quick", i) if quick == 2 else "usual"
        R_ = ee[:, 2, i, :] if quick == 2 else raw[:, :]
        if not (quick == 2 and i):
            raw_free.clear()
        r = act(lambda e: e.copy(R_, pG[:, :]), t, last.get(k_), s="s_raw")
        g_free[0] = r
        later(lambda: qk_rotate(unit, side, i, r, k_, quick), r)

    def qk_rotate(unit, side, i, r, k_, quick):
        i = i if quick == 2 else 0
        P = parts[i]
        raw_, sh_ = (ee[:, 2, i, :], ee[:, 2, 2 + i, :]) if quick == 2 else (raw[:, :], sh[:, :])
        s_ = dve(lambda e: e.stream_shuffle(sh_, raw_, SWAP), r, last.get(k_), s="s_sh", cost=620)
        on, sem = (dve, "s_link") if quick else (pool, "s_rope")
        before = [s_]

        def step(cost, fn, *w):
            before[0] = on(fn, before[0], *w, s=sem, cost=cost)

        steps = [lambda: step(1250, lambda e: e.tensor_tensor(raw_, raw_, rope[:, 0, :], ALU.mult), l_rope),
                 lambda: step(1250, lambda e: e.tensor_tensor(sh_, sh_, rope[:, 1, :], ALU.mult)),
                 lambda: step(1880, lambda e: e.tensor_tensor(P[:, 0, :], raw_, sh_, ALU.add), last["parts"][i]),
                 lambda: step(1250, lambda e: e.tensor_tensor(raw_, raw_, sh_, ALU.add)),
                 lambda: step(1880, lambda e: e.tensor_tensor(P[:, 1, :], raw_, P[:, 0, :], ALU.subtract)),
                 lambda: step(1250, lambda e: e.tensor_tensor(raw_, raw_, P[:, 0, :], ALU.subtract)),
                 lambda: step(1880, lambda e: e.tensor_tensor(P[:, 2, :], raw_, P[:, 1, :], ALU.subtract))]

        def some(steps):
            while steps and (quick or q.free["gpsimd"] <= clock() + AHEAD):
                if len(steps) == 5 and i == 0:
                    if not parts_free:
                        break
                    parts_free.clear()
                steps.pop(0)()
            if steps:
                return later(lambda: some(steps))
            last[k_] = before[0]
            if i == 0:
                raw_free.append(before[0])
            later(lambda: parts_out(unit, side, i, before[0]), before[0])

        some(steps)

    raw_free, parts_free = [None], [None]
    quick_done = []

    def parts_out(unit, side, i, a):
        b, half_ = unit // 2, unit % 2
        P = parts[i]
        hs_ = slice(half_ * 8, half_ * 8 + 8)
        for p in range(3):
            w = dma(d_part[b % 2][side, p, hs_].rearrange("h d t -> (h d) t"), P[:, p, :], a, qk_in.get(unit - 4),
                    s=f"p_w{i}")
        last["parts"][i] = w
        part_in[unit, side] = w
        if i == 0:
            parts_free.append(w)
        if unit < 2:
            quick_done.append(w)

    def assemble(unit):
        free = st_done.get(unit - 3)
        bias_rows(unit, free)
        hs_ = slice((unit % 2) * 8, (unit % 2) * 8 + 8)
        for side in range(2):
            dst = (qa, ka)[side][unit % 3]
            for n, p in enumerate((QPART, KPART)[side]):
                qk_in[unit] = dma(dst[16 * n:16 * n + 16, :, :],
                                  d_part[unit // 2 % 2][side, p, hs_].rearrange("h d t -> d h t"),
                                  part_in[unit, side], free, s=f"qk_in{unit % 3}")

    def assemble_when(unit):
        if (unit, 1) in part_in:
            return assemble(unit)
        later(lambda: assemble_when(unit))

    def v_tiles(b, j):
        for t in range(2):
            for c in range(2):
                yield 427
                tk = pe(lambda e, c=c, t=t: e.matmul(pG[:, t * C:(t + 1) * C],
                                                     xT[:, c, (2 * j + t) * 128:(2 * j + t + 1) * 128],
                                                     wqkv[:, c, 512:768], start=(c == 0), stop=(c == 1)),
                        xT_in_of[b], g_free[0], s="s_g" if (t and c) else None)
        r = act(lambda e: e.copy(vv[b % 2][:, 2 * j:2 * j + 2, :, 0:16],
                                 pG[:, :].rearrange("p (k h d) -> p k h d", k=2, h=H)),
                tk, pv_done.get(4 * (b - 2) + 3), ones, s="s_v")
        g_free[0] = r
        v_ready[b] = r
        xT_read(b, tk)

    xT_left = [6] * NB

    def xT_read(b, tk):
        xT_left[b] -= 1
        if xT_left[b] == 0 and b + 1 < NB:
            xT_in_of[b + 1] = load_xT(b + 1, tk)

    xT_in_of = Done({0: xT_in})
    qk_in, part_in = Done(), Done()
    pv_done = Done()
    xr_in = Done({0: x_in})

    s_max, s_exp, s_ev = Done(), Done(), Done()
    m_in = Done()

    def s_tile(s):
        b, h, t = s // 64, (s // 4) % 16, s % 4
        unit, hu = s // 32, h % 8
        bank = pS[s % 2]
        qs = slice(t * 128, t * 128 + 128)
        pe(lambda e: e.matmul(bank[:, :], qa[unit % 3][0:114, hu, qs], ka[unit % 3][0:114, hu, :], start=True, stop=False),
           qk_in[unit], l_ind[-1], s_max.get(s - 2))
        tk = pe(lambda e: e.matmul(bank[:, qs], tri[:, 1, :], mB[:, h, :], start=False, stop=True), s_const,
                s="s_s")
        g, j = s // 16, (s // 4) % 4
        s_max[s] = dve(lambda e: e.tensor_reduce(negm[:, g % 2, j, t:t + 1], bank[:, :], AX, ALU.max, negate=True),
                       tk, m_split.get(g - 2), s="s_max", cost=640)
        if s % 16 == 15:
            later(lambda: m_rows(g))

    m_split, m_turned, m_out = Done(), Done(), Done()

    def m_rows(g):
        i = g % 2
        a = dve(lambda e: e.tensor_copy(mp[:, i, :, 0, :], negm[:, i, :, :]), s_max[16 * g + 15],
                m_turned.get(g - 2), s="s_mp")
        a = m_split[g] = dve(lambda e: e.tensor_tensor(mp[:, i, :, 1, :], negm[:, i, :, :], mp[:, i, :, 0, :],
                                                       ALU.subtract), a, s="s_mp")
        a = m_turned[g] = dve(lambda e: e.transpose(mT[:, i, :], mp[:, i, :, :, :].rearrange("p h a t -> p (h a t)")),
                              a, m_out.get(g - 2), s="s_mT")
        w = dma(d_m[i].rearrange("a h p t i -> (a h p t) i"), mT[:, i, :], a, m_in.get(g - 2), s=f"m_w{i}")
        m_out[g] = w
        later(lambda: m_rows_in(g, w), w)

    def m_rows_in(g, w):
        i = g % 2
        u, h0 = g // 2, (g % 2) * 4
        for j in range(4):
            m_in[g] = dma(qa[u % 3][114:116, h0 + j, :].rearrange("p (t a i) -> p t a i", t=4, a=4),
                          d_m[i][:, j].rearrange("a p t i -> p t a i"), w, st_done.get(u - 3), s=f"m_in{i}")

    def st_tile(u):
        g, kt, hh = u // 16, (u % 16) // 4, u % 4
        b, h = g // 4, (g % 4) * 4 + hh
        assert len(quick_done) == 4
        unit, hu = u // 32, h % 8
        bank = pT[u % 2]
        ks = slice(kt * 128, kt * 128 + 128)
        pe(lambda e: e.matmul(bank[:, :], ka[unit % 3][0:ROWS, hu, ks], qa[unit % 3][0:ROWS, hu, :], start=True, stop=False),
           m_in[g], s_exp.get(u - 2), s_mA[1])
        for p in range(2):
            tk = pe(lambda e, p=p: e.matmul(bank[:, ks], tri[:, 0, :], mA[:, p, h, :], start=False, stop=(p == 1)),
                    s="s_t" if p else None)
        if u % 32 == 31:
            st_done[unit] = tk
        w = u // 4
        s_exp[u] = act(lambda e: e.activation(ee[:, w % 3, hh, :], bank[:, :], ACT.Exp, scale=0.25), tk,
                       pv_quad.get(w - 3), g4, *(quick_done if u < 12 else ()), s="s_exp")

    pv_quad = Done()
    rec_done = Done()
    att_done = Done()

    def pv_step(w):
        g, kt = w // 4, w % 4
        b = g // 4
        for hh in range(4):
            h = (g % 4) * 4 + hh
            tk = pe(lambda e, hh=hh, h=h: e.matmul(pV[32 * hh:32 * hh + 32, :], vv[b % 2][:, kt, h, :],
                                                   ee[:, w % 3, hh, :], start=(kt == 0), stop=(kt == 3)),
                    s_exp[4 * w + 3], v_ready[b], s_ev.get(g - 1), s="s_pv" if hh == 3 else None)
        pv_quad[w] = tk
        if kt == 3:
            pv_done[g] = tk
            s_ev[g] = act(lambda e: e.copy(pvs[:, g % 5, :], pV[:, :]), tk, proj_done.get((g - 5) // 4), s="s_ev")
            sums_out(g)

    proj_done = Done()

    def sums_out(g):
        i = g % 2
        a = dma(d_sum[i][:, :], pvs[16:128:32, g % 5, :], s_ev[g], sum_in.get(g - 2), s=f"sum_w{i}")
        later(lambda: sums_in(g, a), a)

    def sums_in(g, a):
        i = g % 2
        sum_in[g] = dma(sc[:, i, :], d_sum[i].rearrange("k (c e) -> (k c) e", e=16), a, rec.get(g - 2),
                        s=f"sum_in{i}")
        later(lambda: reciprocals(g), sum_in[g])

    sum_in, rec, rec_w = Done(), Done(), Done()

    def reciprocals(g):
        i = g % 2
        a = rec[g] = dve(lambda e: e.reciprocal(scr[:, i, :], sc[:, i, :]), sum_in[g], rec_w.get(g - 2), s="s_rec")
        a = rec_w[g] = dma(d_rec[i].rearrange("k (c e) -> (k c) e", e=16), scr[:, i, :], a, rec_done.get(g - 2),
                           s=f"rec_w{i}")
        later(lambda: reciprocals_in(g, a), a)

    def reciprocals_in(g, a):
        i = g % 2
        for hh in range(4):
            rec_done[g] = dma(rb[32 * hh:32 * hh + 32, i, :], d_rec[i][hh:hh + 1].broadcast_to([32, T]), a,
                              att_done.get(g - 2), s=f"rec_in{i}")
        later(lambda: scale_att(g), rec_done[g])

    def scale_att(g):
        i = g % 5
        att_done[g] = dve(lambda e: e.tensor_tensor(pvs[:, i, :], pvs[:, i, :], rb[:, g % 2, :], ALU.mult), rec_done[g],
                          s="s_att", cost=640)
        if g % 4 == 3:
            push(lambda: (att_done[g], xr_in[g // 4]), proj_job, g // 4, 0)

    z_in = Done()
    out_w = Done()

    def proj_job(b, j):
        for t in range(2):
            for g in range(4):
                yield 427
                tk = pe(lambda e, t=t, g=g: e.matmul(pG[:, t * C:(t + 1) * C],
                                                     pvs[:, (4 * b + g) % 5,
                                                         (2 * j + t) * 128:(2 * j + t + 1) * 128],
                                                     wp[:, g, :], start=(g == 0), stop=(g == 3)),
                        att_done[4 * b + 3], l_w, g_free[0], s="s_g" if (t and g == 3) else None)
        if j == 1:
            proj_done[b] = tk
        early(lambda: residual(b, j, tk))
        if j == 0:
            push(lambda: (z_in[b, 0],), proj_job, b, 1)
        else:
            later(lambda: norm1_stats(b), tk)

    def residual(b, j, tk):
        zz = z[:, 2 * j:2 * j + 2, :].rearrange("p t c -> p (t c)")
        z_in[b, j] = dve(lambda e: e.tensor_tensor(zz, pG[:, :], zz, ALU.add), tk, xr_in[b], s="s_z",
                           cost=640)
        g_free[0] = z_in[b, j]
        for t in (2 * j, 2 * j + 1):
            stats[b, 0, t] = dve(lambda e, t=t: e.bn_stats(st[:, 0, t, :], z[:, t, :]), z_in[b, j], s="s_st", cost=350)

    stats = Done()

    def rstd(b, k):
        a = None
        for t in range(4):
            a = dve(lambda e, t=t: e.bn_aggr(mv[:, k, t, :], st[:, k, t, :]), stats[b, k, t], s="s_st", cost=350)
        a = link(lambda e: e.tensor_scalar(ve[:, k, :], mv[:, k, :, 1], EPS, None, ALU.add), a)
        return pool(lambda e: e.tensor_tensor(rs[:, k, :], ve[:, k, :], half[:, 0, 0:4], ALU.pow), a, s_half,
                    s="s_pow")

    def norm1_stats(b):
        x1_rs[b] = rstd(b, 0)
        later(lambda: norm1(b), x1_rs[b])

    def norm1(b):
        if b > 1 and b - 2 not in out_w:
            return later(lambda: norm1(b))
        if b > 1 and q.time[out_w[b - 2]] > clock():
            return later(lambda: norm1(b), out_w[b - 2])
        a = x1_rs[b]
        for t in range(4):
            n = dve(lambda e, t=t: e.tensor_scalar(x1[b % 2][:, t, :], z[:, t, :], mv[:, 0, t, 0:1], rs[:, 0, t:t + 1],
                                                   ALU.subtract, ALU.mult), a, s_w1[0], out_w.get(b - 2), s="s_x1", cost=200)
        x1_in[b] = n
        if b + 1 < NB:
            xr_in[b + 1] = load_x(b + 1, n)
        push(lambda: (n, up_done.get(b - 1)), turn_job, b, 0)

    x1_rs, x1_in, x1T_in, ffn_read = Done(), Done(), Done(), Done()

    def turn_job(b, c):
        for t in range(4):
            yield 178
            tk = pe(lambda e, t=t: e.transpose(pG[:, t * 128:t * 128 + 128], x1[b % 2][:, t, c * 128:c * 128 + 128],
                                               idf[:, :]), x1_in[b], g_free[0], s="s_g" if t == 3 else None)
        r = act(lambda e: e.copy(x1T[0][:, c, :].bitcast(F32R), pG[:, :]), tk, up_done.get(b - 1), s="s_x1T")
        r = dve(lambda e: e.tensor_tensor(x1T[1][:, c, :].bitcast(F32R), pG[:, :], x1T[0][:, c, :], ALU.subtract),
                r, s="s_x1l", cost=640)
        g_free[0] = r
        x1T_in[b] = r
        if c == 1:
            for t in range(4):
                r = pool(lambda e, t=t: e.tensor_tensor(x1[b % 2][:, t, :], x1[b % 2][:, t, :], sb2[:, :], ALU.add), tk, l_w,
                         s="s_x1b")
            x1b[b] = r
            push(lambda: (x1T_in[b],), route_job, b)
            push(lambda: (x1T_in[b], down.get(9 * b - 2)), up_job, b, 0)
        else:
            push(lambda: (), turn_job, b, 1)

    x1b = Done()

    def route_job(b):
        yield 960
        for n in range(4):
            for t in range(4):
                tk = pe(lambda e, t=t, n=n: e.matmul(pG[32 * t:32 * t + 32, 0:128], rw[:, n // 2, :],
                                                     x1T[n % 2][:, n // 2, t * 128:t * 128 + 128], start=(n == 0),
                                                     stop=(n == 3)),
                        x1T_in[b], g_free[0], s="s_g" if (t == 3 and n == 3) else None)
        push(lambda: (lg_in[b],), route_turn, b)
        g_free[0] = lg_in[b] = act(lambda e: e.copy(lgT[:, :], pG[:, 0:128]), tk, lg_read.get(b - 1), s="s_lgT")

    def route_turn(b):
        yield 180
        tk = pe(lambda e: e.transpose(pG[:, 0:128], lgT[:, :], idf[:, :]), lg_in[b], g_free[0], s="s_g")
        lg_read[b] = tk
        early(lambda: route_logits(b, tk))

    def route_logits(b, tk):
        a = link(lambda e: e.tensor_tensor(R(0), pG[:, 0:128].rearrange("p (t e) -> p t e", t=4)[:, :, 0:E],
                                           ebb[:, :, :], ALU.add), tk, cp_read.get(b - 1))
        g_free[0] = a
        a = link(lambda e: e.tensor_scalar(R(1), R(0), -1.0, None, ALU.mult), a)
        a = link(lambda e: e.tensor_tensor(R(2), R(0), R(1), ALU.min), a)
        a = act(lambda e: e.activation(R(3), R(2), ACT.Exp), a, s="s_u")
        route_u[b] = a
        later(lambda: route_softplus(b), a)

    lg_in, lg_read = Done(), Done()

    def R(i):
        return rr[:, i, :, :]

    def RB(i):
        return rm[:, i, :].rearrange("p (t a) -> p t a", a=1).broadcast_to([128, 4, E])

    route_u, cp_read, route_a, route_c = Done(), Done(), Done(), Done()

    def route_softplus(b):
        a = link(lambda e: e.tensor_scalar(R(1), R(3), 2.0, None, ALU.add), route_u[b])
        a = link(lambda e: e.reciprocal(R(2), R(1)), a)
        a = link(lambda e: e.tensor_scalar(R(1), R(0), 0.0, None, ALU.max), a)
        todo = [lambda e: e.tensor_tensor(R(4), R(3), R(2), ALU.mult),
                lambda e: e.tensor_tensor(R(5), R(4), R(4), ALU.mult),
                lambda e: e.tensor_scalar(R(6), R(5), 1.0 / 17, None, ALU.mult)]
        todo += [lambda e, n=n: e.scalar_tensor_tensor(R(6), R(6), 1.0 / n, R(5), ALU.add, ALU.mult)
                 for n in (15, 13, 11, 9, 7, 5, 3)]
        todo += [lambda e: e.scalar_tensor_tensor(R(6), R(6), 1.0, R(4), ALU.add, ALU.mult),
                 lambda e: e.scalar_tensor_tensor(R(6), R(6), 2.0, R(1), ALU.mult, ALU.add)]

        def done(a):
            route_a[b] = pool(lambda e: e.tensor_tensor(R(7).rearrange("p t e -> p (t e)"),
                                                        R(6).rearrange("p t e -> p (t e)"), half[:, 1, :], ALU.pow),
                              a, s="s_pow", cost=5300)
            later(lambda: route_top2(b), route_a[b])

        chain(todo, a, done)

    def chain(todo, a, done):
        for fn in todo[:LINKS]:
            a = link(fn, a)
        if todo[LINKS:]:
            later(lambda: chain(todo[LINKS:], a, done))
        else:
            done(a)

    def route_top2(b):
        todo = []
        for n, src in ((0, 7), (1, 11)):
            todo += [lambda e, src=src: e.tensor_reduce(rm[:, 0, :], R(src), AX, ALU.max),
                     lambda e, src=src: e.tensor_tensor(R(1), R(src), RB(0), ALU.is_equal),
                     lambda e: e.tensor_tensor(R(2), R(1), wkey[:, :, :], ALU.mult),
                     lambda e: e.tensor_reduce(rm[:, 1, :], R(2), AX, ALU.max),
                     lambda e, n=n: e.tensor_tensor(R(8 + n), R(2), RB(1), ALU.is_equal)]
            if n == 0:
                todo.append(lambda e: e.scalar_tensor_tensor(R(11), R(8), -1e30, R(7), ALU.mult, ALU.add))
        todo += [lambda e: e.tensor_tensor(R(10), R(8), R(9), ALU.add),
                 lambda e: e.scalar_tensor_tensor(R(10), R(10), 0.5, R(7), ALU.mult, ALU.mult)]

        def done(a):
            route_c[b] = a
            push(lambda: (a, ffn_read.get(b - 1)), cT_job, b)

        chain(todo, route_a[b], done)

    cT_in = Done()

    def cT_job(b):
        for t in range(4):
            yield 178
            tk = pe(lambda e, t=t: e.transpose(pG[0:E, t * 128:t * 128 + 128], R(10)[:, t, :], idf[:, :]),
                    route_c[b], g_free[0], s="s_g" if t == 3 else None)
        cp_read[b] = tk
        r = act(lambda e: e.copy(cT[:, :], pG[0:E, 0:T]), tk, ffn_read.get(b - 1), s="s_cT")
        g_free[0] = r
        w = dma(d_comb, cT[:, :], r, s="comb_w")
        later(lambda: (cf_load(b, 1, w), cf_load(b, 2, w)), w)
        comb_w[b] = w
        push(lambda: (cf_in[9 * b + 1] and None, down[9 * b - 1 if b else 0]), up_job, b, 1)

    def cf_load(b, e_, w):
        n = 9 * b + e_
        cf_in[n] = dma(cf[:, e_ % 2, :], d_comb[e_ - 1:e_].broadcast_to([128, T]), w, b_w,
                       a_done.get(n - 2 if e_ > 2 else n - 3),
                       s=f"cf_in{e_ % 2}")

    up_done, th_in = Done(), Done()
    a_done, comb_w, cf_in, hs_in, down = Done(), Done(), Done(), Done(), Done()

    def up_job(b, e_):
        n = 9 * b + e_
        for c in range(2):
            yield 650
            for k, (i, j) in enumerate(((0, 0), (0, 1), (1, 0))):
                tk = pe(lambda e, c=c, i=i, j=j, k=k: e.matmul(pG[:, :], w1[i][:, e_, c, :].bitcast(F32R),
                                                               x1T[j][:, c, :].bitcast(F32R),
                                                               start=(c == 0 and k == 0), stop=(c == 1 and k == 2)),
                        x1T_in[b], s_w1[0], g_free[0], s="s_g" if (c and k == 2) else None)
        a = act(lambda e: e.activation(zb[:, :], pG[:, :], ACT.Identity, bias=b1[:, e_:e_ + 1]), tk, l_w,
                a_done.get(n - 1), th_in.get(n - 1), s="s_zb")
        g_free[0] = a
        r = act(lambda e: e.activation(th[:, :], zb[:, :], ACT.Tanh, scale=0.5), a, s_w1[0], hs_in.get(n - 1),
                s="s_th")
        th_in[n] = r
        later(lambda: gate(b, e_, a, r), max((r, cf_in[n] if e_ else r), key=q.time.get))
        push(lambda: (hs_in[n], z2_in.get(b - 1)), down_job, b, e_)
        if 0 < e_ < 8:
            push(lambda: (cf_in[n + 1] and a_done[n], down[n - 1]), up_job, b, e_ + 1)
        if e_ == 8:
            up_done[b] = tk

    def gate(b, e_, a, r):
        n = 9 * b + e_
        h_ = hs[n % 2]
        if e_ == 0:
            a = dve(lambda e: e.tensor_scalar(h_[:, :], zb[:, :], 0.5, None, ALU.mult), a, down.get(n - 2),
                    s="s_a", cost=350)
        else:
            a = dve(lambda e: e.tensor_tensor(h_[:, :], zb[:, :], cf[:, e_ % 2, :], ALU.mult), a, cf_in[n],
                    down.get(n - 2), s="s_a", cost=600)
        a_done[n] = a
        if 0 < e_ < 7:
            later(lambda: cf_load(b, e_ + 2, comb_w[b]))
        hs_in[n] = dve(lambda e: e.scalar_tensor_tensor(h_[:, :], th[:, :], 1.0, h_[:, :], ALU.add, ALU.mult),
                       a, r, s="s_hs", cost=620)

    z2_in = Done()

    def down_job(b, e_):
        n = 9 * b + e_
        for t in range(4):
            yield 427
            tk = pe(lambda e, t=t: e.matmul(pD[t // 2][:, t % 2, :], hs[n % 2][:, t * 128:t * 128 + 128],
                                            w2[:, e_, :], start=(e_ == 0 and t % 2 == 0), stop=False,
                                            skip_group_check=True),
                    hs_in[n], z2_in.get(b - 1), s="s_d" if t == 3 else None)
        down[n] = tk
        if e_ == 8:
            for t in range(4):
                yield 427
                tk = pe(lambda e, t=t: e.matmul(pD[t // 2][:, t % 2, :], cT[:, t * 128:t * 128 + 128], rb2[:, :],
                                                start=False, stop=True, skip_group_check=True),
                        s_w[0], s="s_d" if t == 3 else None)
            ffn_read[b] = tk
            early(lambda: residual2(b, tk, 0))
            later(lambda: residual2(b, tk, 1), tk)
            later(lambda: norm2_stats(b), tk)

    def residual2(b, tk, j):
        xx = x1[b % 2][:, 2 * j:2 * j + 2, :].rearrange("p t c -> p (t c)")
        z2_in[b] = dve(lambda e: e.tensor_tensor(xx, pD[j][:, :, :].rearrange("p t c -> p (t c)"), xx, ALU.add),
                       tk, x1b[b], s="s_z2", cost=640)
        for t in (2 * j, 2 * j + 1):
            stats[b, 1, t] = dve(lambda e, t=t: e.bn_stats(st[:, 1, t, :], x1[b % 2][:, t, :]), z2_in[b],
                                 s="s_st", cost=350)

    def norm2_stats(b):
        x2_rs[b] = rstd(b, 1)
        later(lambda: norm2(b), x2_rs[b])

    x2_rs = Done()

    def norm2(b):
        a = x2_rs[b]
        for t in range(4):
            n = dve(lambda e, t=t: e.tensor_scalar(x1[b % 2][:, t, :], x1[b % 2][:, t, :], mv[:, 1, t, 0:1], rs[:, 1, t:t + 1],
                                                   ALU.subtract, ALU.mult), a, s="s_o", cost=200)
        out_w[b] = dma(out[b].rearrange("(t p) c -> p t c", p=128), x1[b % 2][:, :, :], n, s="out_w")

    slot, number = [-1], [0]
    first, soon, ready, running = [], [], [], []
    g_from = [0]

    def clock():
        return q.free["tensor"]

    def early(fn):
        first.append(fn)

    def later(fn, after=None):
        soon.append((slot[0] + 1, after, fn))

    def push(after, fn, *a):
        number[0] += 1
        ready.append((slot[0] + 1, after, number[0], fn, a))

    def passed(after, slack=0):
        return after is None or q.time[after] <= clock() + slack

    def rank(j):
        if j[3] in (down_job, turn_job, route_job, route_turn, cT_job):
            return (0, j[2])
        return (2 if j[3] in (qk_tile, v_tiles) and slot[0] < j[0] + URGENT else 1, j[2])

    def can(j):
        if j[0] > slot[0] or (j[3] != down_job and g_from[0] > slot[0]):
            return False
        try:
            return all(passed(t, SLACK) for t in j[1]())
        except KeyError:
            return False

    def spend(budget):
        while budget > 0:
            if not running:
                j = min((j for j in ready if can(j)), key=rank, default=None)
                if j is None:
                    return 0
                ready.remove(j)
                job = j[3](*j[4])
                running.extend((j[3], job, next(job)))
            fn, job, cost = running
            budget -= cost
            piece[0] = cost
            try:
                running[2] = next(job)
            except StopIteration:
                running.clear()
                if fn != down_job:
                    g_from[0] = slot[0] + 1
        return budget

    def turn():
        slot[0] += 1
        share[0] = 0
        while first:
            first.pop(0)()

    def settle():
        for j in list(soon):
            if j[0] <= slot[0] and share[0] < SHARE and passed(j[1]):
                soon.remove(j)
                j[2]()

    def qk_after(b, quick):
        return (xT_in_of[b],) if quick == 2 else (xT_in_of[b], raw_free[0] if raw_free else {}[0])

    def push_qkv(b, quick=0, halves=(0, 1)):
        for half_ in halves:
            for side in range(2):
                push(lambda: qk_after(b, quick), qk_tile, b, half_, side, quick)

    def push_v(b):
        for j in range(2):
            push(lambda: (xT_in_of[b], pv_done.get(4 * (b - 2) + 3)), v_tiles, b, j)

    push_qkv(0, 2, halves=(0,))
    while ready or running or soon:
        turn()
        settle()
        spend(1e9)
        q.free["tensor"] += 500
    assemble(0)
    push_qkv(0, 2, halves=(1,))
    push_v(0)
    later(weights)
    plan = {}

    def at(s, fn, *a):
        plan.setdefault(s, []).append((fn, a))

    at(20, assemble_when, 1)
    for b in range(NB - 1):
        for h_ in range(2):
            at(64 * b + QK_AT if b else 3, push_qkv, b + 1, 0 if b else h_, (h_,))
        at(64 * b + V_AT, push_v, b + 1)
        at(64 * b + 54, assemble_when, 2 * b + 2)
        at(64 * b + 62, assemble_when, 2 * b + 3)

    def held(s):
        u, v = s - LAG, s - LAG - PVLAG
        w = v // 4
        step = v >= 0 and v % 4 == 0 and w < NTILE // 4
        return (s < NTILE and s // 32 not in qk_in or 0 <= u < NTILE and u // 16 not in m_in
                or step and w // 16 not in v_ready or step and w % 4 == 3 and w >= 20 and (w // 4 - 5) // 4 not in proj_done)

    credit, s, late = 0, 0, 0
    while s < NTILE + LAG + PVLAG or ready or running or soon or first:
        turn()
        start = clock()
        go = not held(s)
        if go and s < NTILE:
            piece[0] = 270
            s_tile(s)
        if go and 0 <= s - LAG < NTILE:
            piece[0] = 330
            st_tile(s - LAG)
        settle()
        v = s - LAG - PVLAG
        credit = min(credit, RATE) + (RATE if running and running[0] in (qk_tile, v_tiles, proj_job) else FAST)
        if go:
            for fn, a in plan.get(s, ()):
                fn(*a)
            if v >= 0 and v % 4 == 0 and v // 4 < NTILE // 4:
                piece[0] = 930
                pv_step(v // 4)
                credit -= 930
            s += 1
        late = 0 if go else late + 1
        assert late < 200
        if s >= NTILE + LAG:
            credit = 3000
        credit = spend(credit)
        if clock() == start:
            q.free["tensor"] += 300
    q.put("sync", None, (out_w[NB - 1],))

    block = ctx.enter_context(nc.Block())

    @block.sync
    def _(e):
        q.run("sync", e)

    @block.tensor
    def _(e):
        q.run("tensor", e)

    @block.vector
    def _(e):
        q.run("vector", e)

    @block.scalar
    def _(e):
        q.run("scalar", e)

    @block.gpsimd
    def _(e):
        q.run("gpsimd", e)


def tables():
    bf = mybir.dt.np(BF16)
    f = np.float32
    t = {}
    inv = (f(1.0) / (f(10000.0) ** (np.arange(0, D, 2, dtype=f) / f(D)))).astype(f)
    fr = (np.arange(T, dtype=f)[:, None] * inv[None, :]).astype(f)
    row = np.arange(128) % D
    t["k_cos"] = np.ascontiguousarray(np.cos(fr).astype(f)[:, row % 8].T)
    sign = np.where(row < 8, f(-1), f(1))[:, None]
    t["k_sin"] = np.ascontiguousarray(np.sin(fr).astype(f)[:, row % 8].T * sign)
    j = np.arange(128)
    t["k_hot"] = (np.arange(128)[:, None] // 8 == np.arange(H)[None, :]).astype(f)
    t["k_tri"] = np.stack([(j[None, :] <= j[:, None]), (j[:, None] < j[None, :])], 1).astype(bf)
    x = np.arange(T)
    kv = np.stack([(x - 128 * (r + 1)) * (x // 128 == r) for r in range(3)])
    qv = np.stack([-(x - 128 * (r + 1)) * (x // 128 > r) for r in range(3)])
    pos = np.stack([kv, qv]).reshape(6, 8, 64).transpose(1, 0, 2).reshape(8, 384)
    t["k_pos"] = np.tile(pos, (16, 1)).astype(f)
    t["k_qind"] = np.repeat(np.stack([x // 128 > r for r in range(3)]), 3, 0).astype(bf)
    t["k_kind"] = np.concatenate([np.repeat(np.stack([x // 128 == r for r in range(3)]), 3, 0),
                                  np.ones((2, T), bool)]).astype(bf)
    t["k_idf"] = np.eye(128, dtype=f)
    t["k_key"] = np.broadcast_to((8 - np.arange(E)).astype(f), (128, 4, E)).copy()
    return t


def kernel(**inputs):
    import concourse.bacc as _bacc
    from concourse.bass_utils import run_bass_kernel_spmd as _run

    i = {n: np.asarray(a) for n, a in inputs.items()}
    x = i["L0_attn_x"]
    a = {"x": x, "xT": x.reshape(NB * T, C).T, "qkv_wT": i["L0_attn_qkv_w"].T, "slopes": i["L0_attn_slopes"]}
    wp = np.zeros((4, 4, 32, C), np.float32)
    wp[:, :, 0:16, :] = i["L0_attn_proj_w"].T.reshape(4, 4, 16, C)
    wp[0, 0, 16, :] = i["L0_attn_proj_b"]
    a["wp"] = wp.transpose(1, 2, 0, 3).reshape(128, 4, C)
    w1 = np.concatenate([i["L0_ffn_sW1"][None], i["L0_ffn_rW1"]])
    a["w1"] = w1.reshape(9, 2, 128, 128).transpose(2, 0, 1, 3)
    a["w2"] = np.concatenate([i["L0_ffn_sW2"][None], i["L0_ffn_rW2"]]).transpose(1, 0, 2)
    a["b1"] = np.concatenate([i["L0_ffn_sb1"][None], i["L0_ffn_rb1"]]).T
    rw = np.zeros((128, 2, 32), np.float32)
    rw[:, :, 0:E] = i["L0_ffn_routing_W"].T.reshape(2, 128, E).transpose(1, 0, 2)
    a["rwT"] = rw
    a["eb"] = i["L0_ffn_expert_bias"]
    a["sb2"] = i["L0_ffn_sb2"]
    a["rb2"] = i["L0_ffn_rb2"]
    a.update(tables())
    nc = _bacc.Bacc("TRN2", target_bir_lowering=False, num_devices=1)
    arrays, aps = {}, {}
    for n, v in a.items():
        v = np.ascontiguousarray(v)
        arrays["in_" + n] = v
        aps[n] = nc.dram_tensor("in_" + n, v.shape, mybir.dt.from_np(v.dtype), kind="ExternalInput").ap()
    out = nc.dram_tensor("out_0", (NB, T, C), F32, kind="ExternalOutput").ap()
    build(nc, aps, out)
    r = _run(nc, [arrays], core_ids=[0])
    return r.results[0]["out_0"]
```
